# Optimizing a Trainium2 kernel written in Bass

```python
import numpy as np
import jax
import jax.numpy as jnp

def _softmax(x, axis=-1):
    return jax.nn.softmax(x, axis=axis)

def _gelu(x):
    return jax.nn.gelu(x, approximate=True)

def _silu(x):
    return jax.nn.silu(x)

def _sigmoid(x):
    return jax.nn.sigmoid(x)

def _layernorm(x, axis=-1, eps=1e-05):
    m = jnp.mean(x, axis=axis, keepdims=True)
    v = jnp.var(x, axis=axis, keepdims=True)
    return (x - m) / jnp.sqrt(v + eps)

def _scatter_add(tgt, idx, src, axis=0):
    return tgt.at[idx].add(src)

def _segment_sum(src, seg, n):
    return jax.ops.segment_sum(src, seg, n)
kernel_name = 'mk_flamingo_gated_d1_seqx_r4_15c073'

def setup_inputs(seed: int=0):
    np.random.seed(seed)
    _w = jnp.asarray

    def _rec_inputs():
        import jax
        import jax.numpy as jnp
        _rk = jax.random.key(seed)
        x = -0.0003929 + 0.9999 * jax.random.normal(jax.random.fold_in(_rk, 1), (4, 1024, 256), jnp.float32)
        _lenS = 1024 - jax.random.randint(jax.random.fold_in(_rk, 7), (4,), 0, max(1, 1024 // 4) + 1, jnp.int32)
        _lenS2 = 77 - jax.random.randint(jax.random.fold_in(_rk, 8), (4,), 0, max(1, 77 // 4) + 1, jnp.int32)
        _ctx_1024P = jax.random.normal(jax.random.fold_in(_rk, 11), (4, 16, 256), jnp.float32)
        _ctx_1024c = jax.random.dirichlet(jax.random.fold_in(_rk, 511), 0.3 * jnp.ones((16,), jnp.float32), (4, 77))
        _ctx_1024t = jnp.einsum('bsk,bkd->bsd', _ctx_1024c, _ctx_1024P)
        _ctx_1024t = _ctx_1024t * jax.lax.rsqrt(jnp.mean(jnp.square(_ctx_1024t)) + 1e-12) * 0.953939
        ctx_1024 = 2.81802e-05 + 1.00001 * (_ctx_1024t + 0.3 * jax.random.normal(jax.random.fold_in(_rk, 611), (4, 77, 256), jnp.float32))
        fside_1xSxS2_0 = 0.000675642 + 1.00031 * jax.random.normal(jax.random.fold_in(_rk, 12), (1, 1024, 77), jnp.float32)
        _g = jax.random.normal(jax.random.fold_in(_rk, 9001), (2, 1), jnp.float32)
        _g = jnp.sign(_g) * jnp.maximum(jnp.abs(_g), 1.0) + (_g == 0) * 1.0
        g_xattn = _g[0]
        g_ffn = _g[1]
        return (x, ctx_1024, fside_1xSxS2_0, g_xattn, g_ffn)
    x, ctx_1024, fside_1xSxS2_0, g_xattn, g_ffn = _rec_inputs()

    def _L0_xattn_setup():
        import jax, jax.numpy as jnp
        import numpy as np
        import math
        D = 256
        B, S = (8, 512)

        def _proj(x, W1, b1, W2, b2):
            h = jnp.einsum('bsd,od->bso', x, W1) + b1
            return jnp.einsum('bsd,od->bso', h, W2) + b2
        key = jax.random.key(seed)
        ks = jax.random.split(key, 8)
        q = jax.random.normal(ks[0], (B, S, D), dtype=jnp.float32)
        k = jax.random.normal(ks[1], (B, S, D), dtype=jnp.float32)
        v1 = jax.random.normal(ks[2], (B, S, D), dtype=jnp.float32)
        mask = jax.random.normal(ks[3], (1, S, S), dtype=jnp.float32)
        lim = 1.0 / math.sqrt(D)
        W1 = jax.random.uniform(ks[4], (D, D), jnp.float32, -lim, lim)
        b1 = jax.random.uniform(ks[5], (D,), jnp.float32, -lim, lim)
        W2 = jax.random.uniform(ks[6], (D, D), jnp.float32, -lim, lim)
        b2 = jax.random.uniform(ks[7], (D,), jnp.float32, -lim, lim)
        return {'q': q, 'k': k, 'v1': v1, 'mask': mask, 'W1': W1, 'b1': b1, 'W2': W2, 'b2': b2}
    _L0_xattn_all = _L0_xattn_setup()
    _L0_xattn_in = {k: v for k, v in _L0_xattn_all.items() if k in ('W1', 'b1', 'W2', 'b2')}
    del _L0_xattn_all

    def _L0_ffn_setup():
        import jax, jax.numpy as jnp
        import numpy as np
        B, S, DIM, FFN, E = (4, 512, 256, 1024, 8)
        key = jax.random.key(seed)
        k0, k1, k2, k3 = jax.random.split(key, 4)
        scale = 0.02
        return {'hidden_states': jax.random.normal(k0, (B, S, DIM), jnp.float32), 'router_w': jax.random.normal(k1, (DIM, E), jnp.float32) * scale, 'router_b': jnp.zeros((E,), jnp.float32), 'w1': jax.random.normal(k2, (E, DIM, 2 * FFN), jnp.float32) * scale, 'w2': jax.random.normal(k3, (E, FFN, DIM), jnp.float32) * scale}
    _L0_ffn_all = _L0_ffn_setup()
    _L0_ffn_in = {k: v for k, v in _L0_ffn_all.items() if k in ('router_w', 'router_b', 'w1', 'w2')}
    del _L0_ffn_all
    return {'x': x, 'ctx_1024': ctx_1024, 'fside_1xSxS2_0': fside_1xSxS2_0, 'g_xattn': g_xattn, 'g_ffn': g_ffn, 'L0_xattn_W1': _L0_xattn_in['W1'], 'L0_xattn_b1': _L0_xattn_in['b1'], 'L0_xattn_W2': _L0_xattn_in['W2'], 'L0_xattn_b2': _L0_xattn_in['b2'], 'L0_ffn_router_w': _L0_ffn_in['router_w'], 'L0_ffn_router_b': _L0_ffn_in['router_b'], 'L0_ffn_w1': _L0_ffn_in['w1'], 'L0_ffn_w2': _L0_ffn_in['w2']}

def reference(x, ctx_1024, fside_1xSxS2_0, g_xattn, g_ffn, L0_xattn_W1, L0_xattn_b1, L0_xattn_W2, L0_xattn_b2, L0_ffn_router_w, L0_ffn_router_b, L0_ffn_w1, L0_ffn_w2):
    import jax
    import jax.numpy as jnp

    def _L0_xattn_ref(q, k, v1, mask, W1, b1, W2, b2):
        import jax, jax.numpy as jnp
        import numpy as np
        import math
        D = 256
        B, S = (8, 512)

        def _proj(x, W1, b1, W2, b2):
            h = jnp.einsum('bsd,od->bso', x, W1) + b1
            return jnp.einsum('bsd,od->bso', h, W2) + b2
        qp = _proj(q, W1, b1, W2, b2)
        kp = _proj(k, W1, b1, W2, b2)
        scale = 1.0 / math.sqrt(qp.shape[-1])
        qk = jnp.einsum('bqd,bkd->bqk', qp, kp) * scale
        qk = qk + mask
        attn = jax.nn.softmax(qk, axis=-1)
        return jnp.einsum('bqk,bkd->bqd', attn, v1)

    def _L0_ffn_ref(hidden_states, router_w, router_b, w1, w2):
        import jax, jax.numpy as jnp
        import numpy as np
        B, S, DIM, FFN, E = (4, 512, 256, 1024, 8)
        b, s, d = hidden_states.shape
        x = hidden_states.reshape(-1, d)
        logits = x @ router_w + router_b
        route = jax.nn.softmax(logits, axis=1)
        max_prob = jnp.max(route, axis=1, keepdims=True)
        max_ind = jnp.argmax(route, axis=1)
        out = jnp.zeros_like(x)
        num_experts = w1.shape[0]
        for e in range(num_experts):
            h = x @ w1[e]
            a, g = jnp.split(h, 2, axis=1)
            y = jax.nn.silu(a) * g @ w2[e]
            out = jnp.where((max_ind == e)[:, None], y, out)
        out = out * max_prob
        return out.reshape(b, s, d)
    x = x + jnp.tanh(g_xattn[0]) * _L0_xattn_ref(_layernorm(x, axis=-1), ctx_1024, ctx_1024, fside_1xSxS2_0, L0_xattn_W1, L0_xattn_b1, L0_xattn_W2, L0_xattn_b2)
    x = x + jnp.tanh(g_ffn[0]) * _L0_ffn_ref(_layernorm(x, axis=-1), L0_ffn_router_w, L0_ffn_router_b, L0_ffn_w1, L0_ffn_w2)
    return x

_drawn_inputs = setup_inputs


def setup_inputs(seed=0):
    import zlib

    import numpy as np

    out = dict(_drawn_inputs(seed))
    spreads = {'L0_ffn_router_b': (0.0, 0.8)}
    factors = {'L0_xattn_b1': 8.0,
     'L0_xattn_W2': 3.224,
     'L0_xattn_b2': 8.0,
     'L0_ffn_router_w': 8.0,
     'L0_ffn_w1': 8.0,
     'L0_ffn_w2': 8.0}
    for name, (base, spread) in spreads.items():
        noise = np.random.default_rng([zlib.crc32(name.encode()), seed]).standard_normal(out[name].shape)
        drawn = base * np.exp(spread * noise) if base else spread * noise
        out[name] = jnp.asarray(drawn.astype(out[name].dtype))
    for name, factor in factors.items():
        out[name] = (out[name] * factor).astype(out[name].dtype)
    return out
```

```python
from contextlib import ExitStack

import concourse.bass as bass
from concourse import mybir

FP32 = mybir.dt.float32
FP32R = mybir.dt.float32r
I32 = mybir.dt.int32
ALU = mybir.AluOpType
ACT = mybir.ActivationFunctionType
AX = mybir.AxisListType

P = 128


def flamingo_block(nc, x, ctx_kv, mask, g_xattn, g_ffn, w1, b1, w2, b2, router_w, router_b, e_w1, e_w2, out):
    B, S, D = x.shape
    KEYS = ctx_kv.shape[1]
    E, _, F2 = e_w1.shape
    F = F2 // 2
    DC = D // P
    NG = S // P
    N = B * S
    NT = N // P
    KB = B * KEYS
    EPS = 1e-5
    SCALE = float(D) ** -0.5
    ROW = D + 2
    MIN_TILES = 3
    PIECES = 3
    PW = F2
    EW = PIECES * PW
    MAXT = NT + MIN_TILES * (E - 1)
    COLS = MAXT + 1
    HALF = 512
    HC = HALF // P
    RES = 4
    XR = 4
    assert DC == 2 and F == 2 * HALF and (F // P) * D == PW and D * F2 == DC * P * PW

    x_groups = x.rearrange("b (s p) d -> s p b d", p=P)
    mask_groups = mask.rearrange("a (s p) k -> p (a s) k", p=P)
    out_rows = out.rearrange("b s d -> (b s) d")
    rows = nc.dram_tensor("residual_rows", (N, ROW), FP32).ap()
    rows_groups = rows.rearrange("(b s p) c -> s p b c", b=B, p=P)
    e_w1_pieces = e_w1.rearrange("e (k p) n -> (e k) p n", p=P)
    e_w2_pieces = e_w2.rearrange("e (c p) n -> e p c n", p=P)

    with ExitStack() as top:
        def buffers(stack, make):
            return lambda name, shape, dt=FP32: stack.enter_context(make(name, shape, dt))

        sb = buffers(top, nc.sbuf_tensor)

        def sem(name):
            return top.enter_context(nc.semaphore(name))

        w_hi = sb("w_hi", [P, 2 * EW], FP32R)
        w_lo = sb("w_lo", [P, 2 * EW], FP32R)
        staging = sb("staging", [P, PIECES * PW])
        ident = sb("ident", [P, P])
        col_of_tile = sb("col_of_tile", [P, COLS])
        tanh_g = sb("tanh_g", [P, 2])
        idx_gather = sb("idx_gather", [P, COLS], I32)
        idx_scatter = sb("idx_scatter", [P, COLS], I32)
        gate_sorted = sb("gate_sorted", [P, COLS])
        last_sorted = sb("last_sorted", [1, 1], I32)
        tile_expert = sb("tile_expert", [1, COLS], I32)
        tile_piece = sb("tile_piece", [1, COLS], I32)

        part1 = ExitStack()
        sb1 = buffers(part1, nc.sbuf_tensor)
        ps1 = buffers(part1, nc.psum_tensor)
        x_in = sb1("x_in", [P, XR, B, D])
        x_row = sb1("x_row", [P, 2, B, ROW])
        mask_in = sb1("mask_in", [P, NG, KEYS])
        mask_c = sb1("mask_c", [P, 2, B, KEYS])
        bias_c = sb1("bias_c", [P, KB])
        keys_t = sb1("keys_t", [P, DC, KB])
        values = sb1("values", [KEYS, B, D])
        router_c = sb1("router_c", [P, DC, E])
        router_b_all = sb1("router_b_all", [P, E])
        bn1 = sb1("bn1", [P, 2, B, 6])
        mv1 = sb1("mv1", [P, 2, B, 2])
        rstd1 = sb1("rstd1", [P, 2, B])
        mr1 = sb1("mr1", [P, 2, B])
        bn2 = sb1("bn2", [P, 2, B, 6])
        mv2 = sb1("mv2", [P, 2, B, 2])
        rstd2 = sb1("rstd2", [P, NG, B])
        var_eps = sb1("var_eps", [P, 2, 2, B])
        minus_half = sb1("minus_half", [P, B])
        q = sb1("q", [P, B, D])
        q_t = sb1("q_t", [P, DC, B * P])
        masked = sb1("masked", [P, B, KEYS])
        neg_max = sb1("neg_max", [P, 2, B])
        probs = sb1("probs", [P, 2, B, KEYS])
        prob_sum = sb1("prob_sum", [P, 2, B])
        prob_inv = sb1("prob_inv", [P, 2, B])
        probs_t = sb1("probs_t", [KEYS, B * P])
        x1_t = sb1("x1_t", [P, DC, B * P])
        logits = sb1("logits", [P, NT, E])

        prep = ExitStack()
        sb0 = buffers(prep, nc.sbuf_tensor)
        ctx_in = sb0("ctx_in", [KEYS, B, D])
        w1_in = sb0("w1_in", [P, DC, D])
        w2_in = sb0("w2_in", [P, DC, D])
        w1_t = sb0("w1_t", [P, DC, D])
        w2_t = sb0("w2_t", [P, DC, D])
        ctx_t = sb0("ctx_t", [P, DC, KB])
        h_t = sb0("h_t", [P, DC, KB])
        b1_in = sb0("b1_in", [P, DC])
        b2_in = sb0("b2_in", [P, DC])
        bq = sb0("bq", [P, DC])
        bq_wide = sb0("bq_wide", [P, DC, P])
        router_in = sb0("router_in", [P, DC, E])
        mean_of = sb0("mean_of", [P, P])
        gates_in = sb0("gates_in", [P, 2])
        kp_t = sb0("kp_t", [P, DC, KB])
        u_t = sb0("u_t", [P, DC, KB])
        prep.close()

        sbr = buffers(part1, nc.sbuf_tensor)
        before = sbr("before", [P, P])
        ones = sbr("ones", [P, P])
        ones_wide = sbr("ones_wide", [P, E * NT])
        slot_iota = sbr("slot_iota", [P, P])
        expert_m8 = sbr("expert_m8", [P, E])
        token_mN = sbr("token_mN", [P, NT])
        onehot = sbr("onehot", [P, E, NT])
        work_a = sbr("work_a", [P, NT, E])
        work_b = sbr("work_b", [P, NT, E])
        best = sbr("best", [P, NT])
        first = sbr("first", [P, NT])
        gate = sbr("gate", [P, NT])
        cum = sbr("cum", [P, E * NT])
        starts = sbr("starts", [P, E + 1])
        counts_i = sbr("counts_i", [P, E], I32)
        tiles_i = sbr("tiles_i", [P, E], I32)
        tiles_f = sbr("tiles_f", [P, E])
        bounds = sbr("bounds", [P, E + 1])
        shift = sbr("shift", [P, E])
        pos_i = sbr("pos_i", [P, 3, NT], I32)
        pos_f = sbr("pos_f", [P, 2, NT])
        slot_hot = sbr("slot_hot", [P, 8, P])
        tile_hot = sbr("tile_hot", [P, 8, 2 * COLS])
        tab_a = sbr("tab_a", [1, COLS, E])
        tab_b = sbr("tab_b", [1, COLS, E])
        tab_e = sbr("tab_e", [1, 4, COLS])

        ps_q = [ps1(f"ps_q{k}", [P, B * P]) for k in range(DC)]
        ps_x = [ps1(f"ps_x{k}", [P, B * P]) for k in range(DC)]
        ps_s = ps1("ps_s", [P, 512])
        ps_p = ps1("ps_p", [P, 512])
        ps_o = ps1("ps_o", [P, 2, D])
        ps_l = ps1("ps_l", [P, 512])
        part1.close()

        part2 = ExitStack()
        sb2 = buffers(part2, nc.sbuf_tensor)
        ps2 = buffers(part2, nc.psum_tensor)
        idx_now = sb2("idx_now", [P, 2], I32)
        x_sorted = sb2("x_sorted", [P, ROW])
        x_norm = sb2("x_norm", [P, D])
        residual = sb2("residual", [P, RES * D])
        xt_hi = sb2("xt_hi", [P, DC, P], FP32R)
        xt_lo = sb2("xt_lo", [P, DC, P], FP32R)
        silu = sb2("silu", [P, 2, HALF])
        hidden = sb2("hidden", [P, 2, HALF])
        ht_hi = sb2("ht_hi", [P, 2, HALF], FP32R)
        ht_lo = sb2("ht_lo", [P, 2, HALF], FP32R)
        out_tile = sb2("out_tile", [P, D])
        pa = [ps2(f"pa{j}", [P, HALF]) for j in range(2)]
        pg = [ps2(f"pg{j}", [P, HALF]) for j in range(2)]
        ph = [ps2(f"ph{j}", [P, HALF]) for j in range(2)]
        py = ps2("py", [P, HALF])
        px = ps2("px", [P, HALF])
        part2.close()

        proj_loaded = sem("proj_loaded")
        misc_loaded = sem("misc_loaded")
        x_loaded = [sem(f"x_loaded{i}") for i in range(XR)]
        rows_stored = [sem(f"rows_stored{i}") for i in range(2)]
        piece_loaded = sem("piece_loaded")
        consts_ready = sem("consts_ready")
        tanh_ready = sem("tanh_ready")
        prep_pe = sem("prep_pe")
        prep_sb = sem("prep_sb")
        prep_dve = sem("prep_dve")
        bn1_ready = sem("bn1_ready")
        mv1_ready = sem("mv1_ready")
        pool_step = sem("pool_step")
        q_ready = sem("q_ready")
        rstd2_ready = sem("rstd2_ready")
        mask_c_ready = sem("mask_c_ready")
        qt_psum = sem("qt_psum")
        qt_ready = sem("qt_ready")
        scores_psum = sem("scores_psum")
        masked_ready = sem("masked_ready")
        max_ready = sem("max_ready")
        probs_ready = sem("probs_ready")
        pt_psum = sem("pt_psum")
        pt_ready = sem("pt_ready")
        inv_ready = sem("inv_ready")
        attn_psum = sem("attn_psum")
        x1_ready = sem("x1_ready")
        bn2_ready = sem("bn2_ready")
        mv2_ready = sem("mv2_ready")
        x1t_psum = sem("x1t_psum")
        x1t_ready = sem("x1t_ready")
        logits_psum = sem("logits_psum")
        logits_ready = sem("logits_ready")
        route_step = sem("route_step")
        route_pool = sem("route_pool")
        centered = sem("centered")
        gate_exp = sem("gate_exp")
        onehot_ready = sem("onehot_ready")
        ranks_psum = sem("ranks_psum")
        pos_ready = sem("pos_ready")
        gate_ready = sem("gate_ready")
        slot_hot_ready = sem("slot_hot_ready")
        tile_hot_ready = sem("tile_hot_ready")
        lists_step = sem("lists_step")
        lists_ready = sem("lists_ready")
        tables_ready = sem("tables_ready")
        w_hi_ready = sem("w_hi_ready")
        w_ready = sem("w_ready")
        idx_now_ready = sem("idx_now_ready")
        gathered = sem("gathered")
        res_ready = sem("res_ready")
        xnorm_ready = sem("xnorm_ready")
        xt_psum = sem("xt_psum")
        xhi_ready = sem("xhi_ready")
        xlo_ready = sem("xlo_ready")
        up_psum = [sem(f"up_psum{j}") for j in range(2)]
        silu_ready = [sem(f"silu_ready{j}") for j in range(2)]
        hidden_ready = [sem(f"hidden_ready{j}") for j in range(2)]
        ht_psum = [sem(f"ht_psum{j}") for j in range(2)]
        hhi_ready = [sem(f"hhi_ready{j}") for j in range(2)]
        hlo_ready = [sem(f"hlo_ready{j}") for j in range(2)]
        down_psum = [sem(f"down_psum{j}") for j in range(2)]
        out_ready = sem("out_ready")
        scattered = sem("scattered")

        HOT = 4
        NB = NT // HOT
        W_CHUNK = PW // 2
        N_CHUNK = PIECES * PW // W_CHUNK

        block = top.enter_context(nc.Block())

        @block.sync
        def _(sp):
            sp.dma_start(ctx_in[:], ctx_kv.rearrange("b k d -> k b d")).then_inc(proj_loaded, 16)
            sp.dma_start(w1_in[:], w1.rearrange("(c p) d -> p c d", p=P)).then_inc(proj_loaded, 16)
            sp.dma_start(w2_in[:], w2.rearrange("(c p) d -> p c d", p=P)).then_inc(proj_loaded, 16)
            with nc.allow_non_contiguous_dma(reason="small vectors"):
                sp.dma_start(b1_in[:], b1.rearrange("(c p) -> p c", p=P)).then_inc(proj_loaded, 16)
                sp.dma_start(b2_in[:], b2.rearrange("(c p) -> p c", p=P)).then_inc(proj_loaded, 16)
            sp.dma_start(x_in[:, 0], x_groups[0]).then_inc(x_loaded[0], 16)
            sp.dma_start(gates_in[:, 0:1], g_xattn.partition_broadcast(P)).then_inc(misc_loaded, 16)
            sp.dma_start(gates_in[:, 1:2], g_ffn.partition_broadcast(P)).then_inc(misc_loaded, 16)
            sp.dma_start(mask_in[:], mask_groups).then_inc(misc_loaded, 16)
            sp.dma_start(router_in[:], router_w.rearrange("(c p) e -> p c e", p=P)).then_inc(misc_loaded, 16)
            sp.dma_start(router_b_all[:], router_b.partition_broadcast(P)).then_inc(misc_loaded, 16)
            for g in range(1, XR):
                sp.dma_start(x_in[:, g], x_groups[g]).then_inc(x_loaded[g], 16)
            for k in range(DC):
                if k:
                    sp.wait_ge(piece_loaded, 16 * k)
                sp.dma_start(staging[:, k * PW:(k + 1) * PW], e_w1_pieces[k]).then_inc(piece_loaded, 16)
            sp.wait_ge(piece_loaded, 16 * DC)
            sp.dma_start(staging[:, DC * PW:EW].rearrange("p (c n) -> p c n", n=D), e_w2_pieces[0]).then_inc(piece_loaded, 16)
            for g in range(NG):
                if g + XR < NG:
                    sp.wait_ge(x1_ready, 2 * (g + 1))
                    sp.dma_start(x_in[:, g % XR], x_groups[g + XR]).then_inc(x_loaded[g % XR], 16)
                sp.wait_ge(rstd2_ready, g + 1)
                sp.dma_start(rows_groups[g], x_row[:, g % 2]).then_inc(rows_stored[g % 2], 16)
            for p in range(PIECES, E * PIECES):
                e, k = divmod(p, PIECES)
                sp.wait_ge(w_ready, p + 1 - PIECES)
                sp.wait_ge(piece_loaded, 16 * p)
                at = staging[:, k * PW:(k + 1) * PW]
                if k < DC:
                    sp.dma_start(at, e_w1_pieces[e * DC + k]).then_inc(piece_loaded, 16)
                else:
                    sp.dma_start(at.rearrange("p (c n) -> p c n", n=D), e_w2_pieces[e]).then_inc(piece_loaded, 16)

        @block.gpsimd
        def _(pool):
            step = [0]

            def link(instruction):
                step[0] += 1
                instruction.then_inc(pool_step, 1)
                pool.wait_ge(pool_step, step[0])

            link(nc.gpsimd.memset(ident[:], 0.0))
            nc.gpsimd.affine_select(out=ident[:], in_=ident[:], compare_op=ALU.not_equal, fill=1.0, base=0,
                                    pattern=[[-1, P]], channel_multiplier=1).then_inc(consts_ready, 1)
            nc.gpsimd.memset(mean_of[:], 1.0 / D)
            nc.gpsimd.memset(minus_half[:], -0.5).then_inc(consts_ready, 1)

            def rstd_of(variance, tmp, result):
                link(nc.gpsimd.tensor_scalar(tmp, variance, EPS, None, ALU.add))
                link(nc.gpsimd.tensor_tensor(out=result, in0=tmp, in1=minus_half[:], op=ALU.pow))

            def norm1(g):
                r = g % 2
                pool.wait_ge(mv1_ready, g + 1)
                rstd_of(mv1[:, r, :, 1], var_eps[:, 0, r], rstd1[:, r])
                link(nc.gpsimd.tensor_tensor(out=mr1[:, r], in0=mv1[:, r, :, 0], in1=rstd1[:, r], op=ALU.mult))
                if g:
                    pool.wait_ge(qt_psum, g)
                for b in range(B):
                    last = nc.gpsimd.tensor_scalar(q[:, b], x_in[:, g % XR, b], rstd1[:, r, b:b + 1],
                                                   mr1[:, r, b:b + 1], ALU.mult, ALU.subtract)
                last.then_inc(q_ready, 1)

            def mask1(g):
                if g == 0:
                    pool.wait_ge(misc_loaded, 80)
                    pool.wait_ge(prep_sb, 12)
                if g >= 2:
                    pool.wait_ge(masked_ready, g - 1)
                nc.gpsimd.tensor_tensor(out=mask_c[:, g % 2], in0=bias_c[:].rearrange("p (b k) -> p b k", b=B),
                                        in1=mask_in[:, g:g + 1, :].to_broadcast([P, B, KEYS]),
                                        op=ALU.add).then_inc(mask_c_ready, 1)

            def norm2(g):
                r = g % 2
                pool.wait_ge(mv2_ready, g + 1)
                rstd_of(mv2[:, r, :, 1], var_eps[:, 1, r], rstd2[:, g])
                nc.gpsimd.tensor_copy(x_row[:, r, :, D + 1], rstd2[:, g])
                nc.gpsimd.tensor_tensor(out=x_row[:, r, :, D], in0=mv2[:, r, :, 0], in1=rstd2[:, g],
                                        op=ALU.mult).then_inc(rstd2_ready, 1)

            def low0(c):
                pool.wait_ge(w_hi_ready, c + 1)
                at = slice(c * W_CHUNK, (c + 1) * W_CHUNK)
                lo = nc.gpsimd.tensor_tensor(out=w_lo[:, at], in0=staging[:, at], in1=w_hi[:, at].bitcast(FP32),
                                             op=ALU.subtract)
                if c % 2:
                    lo.then_inc(w_ready, 1)

            norm1(0)
            for i in range(1, NG + 2):
                if i - 1 < NG:
                    mask1(i - 1)
                if i < NG:
                    norm1(i)
                if 0 <= i - 2 < NG:
                    norm2(i - 2)
                if 0 <= i - 2 < N_CHUNK:
                    low0(i - 2)

            rstep = [0]

            def rlink(instruction):
                rstep[0] += 1
                instruction.then_inc(route_pool, 1)
                pool.wait_ge(route_pool, rstep[0])

            rlink(nc.gpsimd.memset(before[:], 1.0))
            nc.gpsimd.affine_select(out=before[:], in_=before[:], compare_op=ALU.is_gt, fill=0.0, base=0,
                                    pattern=[[1, P]], channel_multiplier=-1)
            nc.gpsimd.memset(ones[:], 1.0)
            nc.gpsimd.memset(ones_wide[:], 1.0)
            nc.gpsimd.iota(slot_iota[:], [[1, P]], base=0, channel_multiplier=0, allow_small_or_imprecise_dtypes=True)
            nc.gpsimd.iota(expert_m8[:], [[1, E]], base=-E, channel_multiplier=0, allow_small_or_imprecise_dtypes=True)
            nc.gpsimd.iota(token_mN[:].rearrange("p (g b) -> p g b", b=B), [[P, NG], [S, B]], base=-N,
                           channel_multiplier=1, allow_small_or_imprecise_dtypes=True)
            nc.gpsimd.iota(col_of_tile[:], [[1, COLS]], base=0, channel_multiplier=0,
                           allow_small_or_imprecise_dtypes=True).then_inc(consts_ready, 1)
            pool.wait_ge(pos_ready, 1)
            pool.wait_ge(consts_ready, 3)
            for n in range(NB):
                if n >= 2:
                    pool.wait_ge(lists_step, n - 1)
                for t in range(n * HOT, (n + 1) * HOT):
                    last = nc.gpsimd.tensor_scalar(slot_hot[:, t % 8], slot_iota[:], pos_f[:, 1, t:t + 1], None,
                                                   ALU.is_equal)
                last.then_inc(slot_hot_ready, 1)

            pool.wait_ge(lists_ready, 2)
            pool.wait_ge(tables_ready, 1)
            for i in range(2):
                pool.wait_ge(rows_stored[i], 16 * (NG // 2))
            last_tile = pool.value_load(last_sorted[0:1, 0:1], min_val=E * MIN_TILES - 1, max_val=MAXT - 1)
            total = pool.snap(last_tile + 1)

            def last_row(t):
                return N - 1 if isinstance(t, int) else pool.snap((t >> 6) + (N - 1))

            def gather(t, now):
                nc.gpsimd.tensor_copy(idx_now[:, 0:1], idx_gather[:, bass.ds(t, 1)]).then_inc(idx_now_ready, 1)
                pool.wait_ge(idx_now_ready, now + 1)
                pool.indirect_dma_start(x_sorted[:], None, rows, bass.IndirectOffsetOnAxis(ap=idx_now[:, 0:1], axis=0),
                                        bounds_check=last_row(t), oob_is_err=False).then_inc(gathered, 16)

            def scatter(t, now):
                pool.wait_ge(out_ready, t + 2)
                nc.gpsimd.tensor_copy(idx_now[:, 1:2], idx_scatter[:, bass.ds(t, 1)]).then_inc(idx_now_ready, 1)
                pool.wait_ge(idx_now_ready, now + 1)
                pool.indirect_dma_start(out_rows, bass.IndirectOffsetOnAxis(ap=idx_now[:, 1:2], axis=0), out_tile[:],
                                        None, bounds_check=last_row(t), oob_is_err=False).then_inc(scattered, 16)

            gather(0, 0)
            pool.wait_ge(xnorm_ready, 1)
            pool.wait_ge(res_ready, 1)
            gather(1, 1)
            with pool.Fori(1, total) as t:
                pool.wait_ge(xnorm_ready, t + 1)
                pool.wait_ge(res_ready, t + 1)
                gather(t + 1, t * 2)
                scatter(t - 1, t * 2 + 1)
            scatter(last_tile, total * 2)
            pool.wait_ge(scattered, total * 16)

        @block.scalar
        def _(act):
            act.wait_ge(misc_loaded, 80)
            nc.scalar.activation(tanh_g[:], gates_in[:], ACT.Tanh).then_inc(tanh_ready, 1)
            act.wait_ge(prep_pe, 1)
            nc.scalar.copy(w1_t[:], ps_q[0][:].rearrange("p (c d) -> p c d", c=DC)).then_inc(prep_sb, 1)
            act.wait_ge(prep_pe, 3)
            nc.scalar.copy(ctx_t[:, 0], ps_x[0][:, 0:KB]).then_inc(prep_sb, 1)
            act.wait_ge(prep_pe, 5)
            nc.scalar.activation(h_t[:, 0], ps_s[:, 0:KB], ACT.Identity, bias=b1_in[:, 0:1]).then_inc(prep_sb, 1)
            act.wait_ge(prep_pe, 6)
            nc.scalar.activation(kp_t[:, 0], ps_q[0][:, 0:KB], ACT.Identity, bias=b2_in[:, 0:1]).then_inc(prep_sb, 1)
            act.wait_ge(prep_pe, 8)
            nc.scalar.copy(u_t[:, 0], ps_x[0][:, 0:KB]).then_inc(prep_sb, 1)
            act.wait_ge(prep_pe, 9)
            nc.scalar.mul(keys_t[:, 0], ps_s[:, 0:KB], SCALE).then_inc(prep_sb, 1)

            def high0(c):
                if c % 2 == 0:
                    act.wait_ge(piece_loaded, 16 * (c // 2 + 1))
                at = slice(c * W_CHUNK, (c + 1) * W_CHUNK)
                nc.scalar.copy(w_hi[:, at], staging[:, at]).then_inc(w_hi_ready, 1)

            def copy_qt(g):
                act.wait_ge(qt_psum, g + 1)
                if g:
                    act.wait_ge(scores_psum, g)
                for k in range(DC):
                    last = nc.scalar.copy(q_t[:, k], ps_q[k][:])
                last.then_inc(qt_ready, 1)

            def copy_pt(g):
                act.wait_ge(pt_psum, g + 1)
                if g:
                    act.wait_ge(attn_psum, 2 * g)
                nc.scalar.copy(probs_t[:], ps_p[0:KEYS, :]).then_inc(pt_ready, 1)

            def copy_x1t(g):
                act.wait_ge(x1t_psum, g + 1)
                if g:
                    act.wait_ge(logits_psum, g)
                for k in range(DC):
                    last = nc.scalar.copy(x1_t[:, k], ps_x[k][:])
                last.then_inc(x1t_ready, 1)

            def softmax(g):
                r = g % 2
                act.wait_ge(max_ready, g + 1)
                if g >= 2:
                    act.wait_ge(pt_psum, g - 1)
                    act.wait_ge(inv_ready, g - 1)
                for b in range(B):
                    last = nc.scalar.activation(probs[:, r, b], masked[:, b], ACT.Exp, bias=neg_max[:, r, b:b + 1],
                                                accum_out=prob_sum[:, r, b:b + 1])
                last.then_inc(probs_ready, 1)

            for i in range(1, NG + 3):
                if i - 1 < NG:
                    copy_qt(i - 1)
                if 0 <= i - 2 < NG:
                    copy_pt(i - 2)
                if 0 <= i - 3 < NG:
                    copy_x1t(i - 3)
                if i - 1 < NG:
                    softmax(i - 1)
                if i - 1 < N_CHUNK:
                    high0(i - 1)

            act.wait_ge(centered, 1)
            nc.scalar.activation(work_b[:], work_b[:], ACT.Exp).then_inc(gate_exp, 1)

            act.wait_ge(tables_ready, 1)
            last_tile = act.value_load(last_sorted[0:1, 0:1], min_val=E * MIN_TILES - 1, max_val=MAXT - 1)
            total = act.snap(last_tile + 1)

            def x_high(t):
                act.wait_ge(xt_psum, t + 1)
                nc.scalar.copy(xt_hi[:], px[:, 0:D].rearrange("p (k n) -> p k n", k=DC)).then_inc(xhi_ready, 1)

            def residual_copy(t):
                act.wait_ge(gathered, t * 16 + 16)
                act.wait_ge(gathered, t * 16 + 16)
                nc.scalar.copy(residual[:, bass.ds((t & (RES - 1)) * D, D)], x_sorted[:, 0:D]).then_inc(res_ready, 1)

            def gate_half(t, j, start):
                act.wait_ge(up_psum[j], t + 1)
                if not start:
                    act.wait_ge(hidden_ready[j], t)
                nc.scalar.activation(silu[:, j], pa[j][:], ACT.Silu).then_inc(silu_ready[j], 1)

            def h_high(t, j, start):
                act.wait_ge(ht_psum[j], t + 1)
                if not start:
                    act.wait_ge(down_psum[j], t)
                nc.scalar.copy(ht_hi[:, j], ph[j][:]).then_inc(hhi_ready[j], 1)

            residual_copy(0)
            x_high(0)

            def tile(t, start):
                gate_half(t, 0, start)
                residual_copy(t + 1)
                act.wait_ge(up_psum[1], t + 1)
                x_high(t + 1)
                gate_half(t, 1, start)
                h_high(t, 0, start)
                piece = act.value_load(tile_piece[0:1, bass.ds(t, 1)], min_val=0, max_val=E * PIECES - 1)
                with act.If(piece > 0):
                    slot = ((piece // PIECES) & 1) * EW
                    src = (piece % PIECES) * PW
                    if not start:
                        act.wait_ge(down_psum[1], t)
                    act.wait_ge(piece_loaded, (piece + 1) * 16)
                    act.wait_ge(piece_loaded, (piece + 1) * 16)
                    nc.scalar.copy(w_hi[:, bass.ds(slot + src, PW)], staging[:, bass.ds(src, PW)]).then_inc(w_hi_ready, 1)
                h_high(t, 1, start)

            tile(0, True)
            with act.Fori(1, total) as t:
                tile(t, False)

        @block.vector
        def _(dve):
            dve.wait_ge(proj_loaded, 80)
            dve.wait_ge(prep_pe, 2)
            nc.vector.tensor_copy(w2_t[:], ps_q[1][:].rearrange("p (c d) -> p c d", c=DC)).then_inc(prep_sb, 1)
            dve.wait_ge(prep_pe, 3)
            nc.vector.tensor_copy(ctx_t[:, 1], ps_x[1][:, 0:KB]).then_inc(prep_sb, 1)
            dve.wait_ge(prep_pe, 5)
            nc.vector.tensor_scalar(h_t[:, 1], ps_p[:, 0:KB], b1_in[:, 1:2], None, ALU.add).then_inc(prep_sb, 1)
            nc.vector.tensor_tensor(out=bq[:], in0=ps_l[:, 0:DC], in1=b2_in[:], op=ALU.add).then_inc(prep_dve, 1)
            dve.wait_ge(prep_dve, 1)
            nc.vector.tensor_copy(bq_wide[:], bq[:].unsqueeze(2).to_broadcast([P, DC, P])).then_inc(prep_dve, 1)
            dve.wait_ge(prep_pe, 6)
            nc.vector.tensor_scalar(kp_t[:, 1], ps_q[1][:, 0:KB], b2_in[:, 1:2], None, ALU.add).then_inc(prep_sb, 1)
            dve.wait_ge(prep_pe, 8)
            nc.vector.tensor_copy(u_t[:, 1], ps_x[1][:, 0:KB]).then_inc(prep_sb, 1)
            dve.wait_ge(prep_pe, 9)
            nc.vector.tensor_scalar(bias_c[:], ps_o[:].rearrange("p a d -> p (a d)")[:, 0:KB], SCALE, None, ALU.mult)
            nc.vector.tensor_scalar(keys_t[:, 1], ps_p[:, 0:KB], SCALE, None, ALU.mult).then_inc(prep_sb, 1)
            dve.wait_ge(tanh_ready, 1)
            nc.vector.tensor_scalar(values[:], ctx_in[:], tanh_g[0:KEYS, 0:1], None, ALU.mult)
            dve.wait_ge(misc_loaded, 80)
            nc.vector.tensor_tensor(out=router_c[:], in0=router_in[:],
                                    in1=ps_l[:, 64:64 + E].unsqueeze(1).to_broadcast([P, DC, E]),
                                    op=ALU.subtract).then_inc(prep_dve, 1)

            def stats1(g):
                r = g % 2
                dve.wait_ge(x_loaded[g % XR], 16 * (g // XR + 1))
                for b in range(B):
                    last = nc.vector.bn_stats(bn1[:, r, b], x_in[:, g % XR, b])
                last.then_inc(bn1_ready, 1)
                dve.wait_ge(bn1_ready, g + 1)
                if g >= 2:
                    dve.wait_ge(q_ready, g - 1)
                for b in range(B):
                    last = nc.vector.bn_aggr(mv1[:, r, b], bn1[:, r, b])
                last.then_inc(mv1_ready, 1)

            def mask_and_max(g):
                r = g % 2
                dve.wait_ge(scores_psum, g + 1)
                dve.wait_ge(mask_c_ready, g + 1)
                if g:
                    dve.wait_ge(probs_ready, g)
                nc.vector.tensor_tensor(out=masked[:], in0=ps_s[:, 0:KB].rearrange("p (b k) -> p b k", b=B),
                                        in1=mask_c[:, r], op=ALU.add).then_inc(masked_ready, 1)
                dve.wait_ge(masked_ready, g + 1)
                nc.vector.tensor_reduce(neg_max[:, r], masked[:], AX.X, ALU.max, negate=True).then_inc(max_ready, 1)

            def invert_sums(g):
                r = g % 2
                dve.wait_ge(probs_ready, g + 1)
                nc.vector.reciprocal(prob_inv[:, r], prob_sum[:, r]).then_inc(inv_ready, 1)
                dve.wait_ge(inv_ready, g + 1)

            def add_attention(g, half):
                r = g % 2
                dve.wait_ge(attn_psum, 2 * g + half + 1)
                if half == 0 and g >= 2:
                    dve.wait_ge(rows_stored[r], 16 * (g // 2))
                    dve.wait_ge(x1t_psum, g - 1)
                for b in range(2 * half, 2 * half + 2):
                    last = nc.vector.scalar_tensor_tensor(out=x_row[:, r, b, 0:D], in0=ps_o[:, b % 2],
                                                          scalar=prob_inv[:, r, b:b + 1], in1=x_in[:, g % XR, b],
                                                          op0=ALU.mult, op1=ALU.add)
                last.then_inc(x1_ready, 1)

            def stats2(g):
                r = g % 2
                dve.wait_ge(x1_ready, 2 * (g + 1))
                for b in range(B):
                    last = nc.vector.bn_stats(bn2[:, r, b], x_row[:, r, b, 0:D])
                last.then_inc(bn2_ready, 1)
                dve.wait_ge(bn2_ready, g + 1)
                if g >= 2:
                    dve.wait_ge(rstd2_ready, g - 1)
                for b in range(B):
                    last = nc.vector.bn_aggr(mv2[:, r, b], bn2[:, r, b])
                last.then_inc(mv2_ready, 1)

            def keep_logits(g):
                dve.wait_ge(logits_psum, g + 1)
                nc.vector.tensor_copy(logits[:, g * B:(g + 1) * B], ps_l[:, 0:B * E].rearrange("p (b e) -> p b e", b=B)
                                      ).then_inc(logits_ready, 1)

            stats1(0)
            for i in range(1, NG + 3):
                if i - 1 < NG:
                    mask_and_max(i - 1)
                if 0 <= i - 2 < NG:
                    invert_sums(i - 2)
                    add_attention(i - 2, 0)
                if i < NG:
                    stats1(i)
                if 0 <= i - 2 < NG:
                    add_attention(i - 2, 1)
                    stats2(i - 2)
                if 0 <= i - 3 < NG:
                    keep_logits(i - 3)

            step = [0]

            def link(instruction):
                step[0] += 1
                instruction.then_inc(route_step, 1)
                dve.wait_ge(route_step, step[0])

            def over_experts(v):
                return v.unsqueeze(2).to_broadcast([P, NT, E])

            def over_tiles(v):
                return v.unsqueeze(1).to_broadcast([P, NT, E])

            dve.wait_ge(logits_ready, NG)
            dve.wait_ge(rstd2_ready, NG)
            link(nc.vector.tensor_tensor(out=work_a[:], in0=logits[:], in1=over_experts(rstd2[:].rearrange("p g b -> p (g b)")),
                                         op=ALU.mult))
            link(nc.vector.tensor_tensor(out=logits[:], in0=work_a[:], in1=over_tiles(router_b_all[:]), op=ALU.add))
            link(nc.vector.tensor_reduce(best[:], logits[:], AX.X, ALU.max))
            nc.vector.tensor_tensor(out=work_b[:], in0=logits[:], in1=over_experts(best[:]), op=ALU.subtract).then_inc(centered, 1)
            link(nc.vector.tensor_tensor(out=work_a[:], in0=logits[:], in1=over_experts(best[:]), op=ALU.is_equal))
            dve.wait_ge(consts_ready, 3)
            link(nc.vector.tensor_tensor(out=work_a[:], in0=work_a[:], in1=over_tiles(expert_m8[:]), op=ALU.mult))
            link(nc.vector.tensor_reduce(first[:], work_a[:], AX.X, ALU.min))
            nc.vector.tensor_tensor(out=onehot[:].rearrange("p e t -> p t e"), in0=over_tiles(expert_m8[:]),
                                    in1=over_experts(first[:]), op=ALU.is_equal).then_inc(onehot_ready, 1)
            dve.wait_ge(gate_exp, 1)
            link(nc.vector.tensor_reduce(best[:], work_b[:], AX.X, ALU.add))
            link(nc.vector.reciprocal(first[:], best[:]))
            link(nc.vector.tensor_scalar(gate[:], first[:], tanh_g[:, 1:2], None, ALU.mult))
            dve.wait_ge(ranks_psum, 1)
            link(nc.vector.tensor_tensor_scan(cum[:], ones_wide[:], ps_q[1][:, 0:E * NT], 0.0, ALU.mult, ALU.add))
            nc.vector.memset(starts[:, 0:1], 0.0)
            nc.vector.memset(bounds[:, 0:1], 0.0)
            link(nc.vector.tensor_copy(starts[:, 1:E + 1], cum[:].rearrange("p (e t) -> p e t", t=NT)[:, :, NT - 1]))
            link(nc.vector.scalar_tensor_tensor(out=counts_i[:], in0=starts[:, 1:E + 1], scalar=float(P - 1),
                                                in1=starts[:, 0:E], op0=ALU.add, op1=ALU.subtract))
            link(nc.vector.tensor_scalar(tiles_i[:], counts_i[:], 7, None, ALU.arith_shift_right))
            link(nc.vector.tensor_scalar(tiles_f[:], tiles_i[:], float(MIN_TILES), None, ALU.max))
            link(nc.vector.tensor_tensor_scan(bounds[:, 1:E + 1], ones_wide[:, 0:E], tiles_f[:], 0.0, ALU.mult, ALU.add))
            link(nc.vector.scalar_tensor_tensor(out=shift[:], in0=bounds[:, 0:E], scalar=float(P), in1=starts[:, 0:E],
                                                op0=ALU.mult, op1=ALU.subtract))
            wa = work_a[:].rearrange("p t e -> p (t e)")
            wa_et = wa.rearrange("p (e t) -> p e t", t=NT)
            link(nc.vector.tensor_tensor(out=wa, in0=cum[:], in1=ps_q[1][:, 0:E * NT], op=ALU.subtract))
            link(nc.vector.tensor_tensor(out=cum[:], in0=wa, in1=ps_q[0][:, 0:E * NT], op=ALU.add))
            link(nc.vector.tensor_tensor(out=wa_et, in0=cum[:].rearrange("p (e t) -> p e t", t=NT),
                                         in1=shift[:].unsqueeze(2).to_broadcast([P, E, NT]), op=ALU.add))
            link(nc.vector.tensor_tensor(out=wa_et, in0=wa_et, in1=onehot[:], op=ALU.mult))
            link(nc.vector.tensor_reduce(first[:], wa_et.rearrange("p e t -> p t e"), AX.X, ALU.add))
            link(nc.vector.tensor_copy(pos_i[:, 0], first[:]))
            nc.vector.tensor_scalar(pos_i[:, 1], pos_i[:, 0], 7, None, ALU.arith_shift_right)
            link(nc.vector.tensor_scalar(pos_i[:, 2], pos_i[:, 0], P - 1, None, ALU.bitwise_and))
            nc.vector.tensor_copy(pos_f[:], pos_i[:, 1:3]).then_inc(pos_ready, 1)
            dve.wait_ge(pos_ready, 1)
            for n in range(NB):
                if n >= 2:
                    dve.wait_ge(lists_step, n - 1)
                for t in range(n * HOT, (n + 1) * HOT):
                    nc.vector.tensor_scalar(tile_hot[:, t % 8, 0:COLS], col_of_tile[:], pos_f[:, 0, t:t + 1],
                                            token_mN[:, t:t + 1], ALU.is_equal, ALU.mult)
                    last = nc.vector.tensor_scalar(tile_hot[:, t % 8, COLS:2 * COLS], col_of_tile[:],
                                                   pos_f[:, 0, t:t + 1], gate[:, t:t + 1], ALU.is_equal, ALU.mult)
                last.then_inc(tile_hot_ready, 1)
            cols = col_of_tile[0:1, :].unsqueeze(2).to_broadcast([1, COLS, E])
            first_tile = bounds[0:1, 0:E].unsqueeze(1).to_broadcast([1, COLS, E])
            link(nc.vector.tensor_tensor(out=tab_a[:], in0=cols, in1=first_tile, op=ALU.is_ge))
            link(nc.vector.tensor_tensor(out=tab_b[:], in0=tab_a[:], in1=first_tile, op=ALU.mult))
            link(nc.vector.tensor_reduce(tab_e[:, 0], tab_a[:], AX.X, ALU.add))
            link(nc.vector.tensor_reduce(tab_e[:, 1], tab_b[:], AX.X, ALU.max))
            link(nc.vector.tensor_tensor(out=tab_e[:, 2], in0=col_of_tile[0:1, :], in1=tab_e[:, 1], op=ALU.subtract))
            link(nc.vector.scalar_tensor_tensor(out=tab_e[:, 3], in0=tab_e[:, 0], scalar=float(PIECES), in1=tab_e[:, 2],
                                                op0=ALU.mult, op1=ALU.add))
            link(nc.vector.scalar_tensor_tensor(out=tab_e[:, 1], in0=tab_e[:, 2], scalar=float(PIECES), in1=tab_e[:, 3],
                                                op0=ALU.is_lt, op1=ALU.mult))
            nc.vector.tensor_scalar(tile_expert[:], tab_e[:, 0], -1.0, None, ALU.add)
            nc.vector.tensor_scalar(last_sorted[:], bounds[0:1, E:E + 1], -1.0, None, ALU.add)
            nc.vector.scalar_tensor_tensor(out=tile_piece[:], in0=tab_e[:, 1], scalar=float(E * PIECES), in1=tab_e[:, 1],
                                           op0=ALU.is_lt, op1=ALU.mult).then_inc(tables_ready, 1)
            dve.wait_ge(lists_step, NB)
            nc.vector.tensor_scalar(idx_gather[:], ps_s[:, 0:COLS], float(N), float(N - 1), ALU.add, ALU.min).then_inc(lists_ready, 1)
            nc.vector.tensor_scalar(idx_scatter[:], ps_s[:, 0:COLS], float(N), None, ALU.add)
            nc.vector.tensor_copy(gate_sorted[:], ps_s[:, COLS:2 * COLS]).then_inc(lists_ready, 1)

            dve.wait_ge(lists_ready, 2)
            last_tile = dve.value_load(last_sorted[0:1, 0:1], min_val=E * MIN_TILES - 1, max_val=MAXT - 1)
            total = dve.snap(last_tile + 1)

            def norm(t):
                dve.wait_ge(gathered, t * 16 + 16)
                if not (isinstance(t, int) and t == 0):
                    dve.wait_ge(xt_psum, t)
                nc.vector.tensor_scalar(x_norm[:], x_sorted[:, 0:D], x_sorted[:, D + 1:D + 2], x_sorted[:, D:D + 1],
                                        ALU.mult, ALU.subtract).then_inc(xnorm_ready, 1)

            def x_low(t):
                dve.wait_ge(xhi_ready, t + 1)
                nc.vector.tensor_tensor(out=xt_lo[:], in0=px[:, 0:D].rearrange("p (k n) -> p k n", k=DC),
                                        in1=xt_hi[:].bitcast(FP32), op=ALU.subtract).then_inc(xlo_ready, 1)

            def multiply(t, j, start):
                dve.wait_ge(silu_ready[j], t + 1)
                if not start:
                    dve.wait_ge(ht_psum[j], t)
                nc.vector.tensor_tensor(out=hidden[:, j], in0=pg[j][:], in1=silu[:, j], op=ALU.mult
                                        ).then_inc(hidden_ready[j], 1)

            def h_low(t, j):
                dve.wait_ge(hhi_ready[j], t + 1)
                nc.vector.tensor_tensor(out=ht_lo[:, j], in0=ph[j][:], in1=ht_hi[:, j].bitcast(FP32),
                                        op=ALU.subtract).then_inc(hlo_ready[j], 1)

            def finish(t):
                if not (isinstance(t, int) and t == 0):
                    dve.wait_ge(scattered, t * 16)
                dve.wait_ge(down_psum[1], t + 1)
                nc.vector.scalar_tensor_tensor(out=out_tile[:], in0=py[:, 0:D], scalar=gate_sorted[:, bass.ds(t, 1)],
                                               in1=residual[:, bass.ds((t & (RES - 1)) * D, D)], op0=ALU.mult,
                                               op1=ALU.add).then_inc(out_ready, 1)

            def tile(t, start):
                multiply(t, 0, start)
                norm(t + 1)
                x_low(t + 1)
                multiply(t, 1, start)
                h_low(t, 0)
                if not start:
                    finish(t - 1)
                piece = dve.value_load(tile_piece[0:1, bass.ds(t, 1)], min_val=0, max_val=E * PIECES - 1)
                with dve.If(piece > 0):
                    slot = ((piece // PIECES) & 1) * EW
                    src = (piece % PIECES) * PW
                    dve.wait_ge(w_hi_ready, piece + (N_CHUNK - PIECES + 1))
                    nc.vector.tensor_tensor(out=w_lo[:, bass.ds(slot + src, PW)], in0=staging[:, bass.ds(src, PW)],
                                            in1=w_hi[:, bass.ds(slot + src, PW)].bitcast(FP32),
                                            op=ALU.subtract).then_inc(w_ready, 1)
                h_low(t, 1)

            dve.sem_inc(out_ready, 1)
            norm(0)
            x_low(0)
            tile(0, True)
            tile(1, False)
            with dve.Fori(2, total) as t:
                tile(t, False)
            finish(last_tile)

        @block.tensor
        def _(pe):
            mm = nc.tensor.matmul
            pe.wait_ge(proj_loaded, 80)
            pe.wait_ge(consts_ready, 1)
            for ps, w in ((ps_q[0], w1_in), (ps_q[1], w2_in)):
                for dc in range(DC):
                    for oc in range(DC):
                        last = nc.tensor.transpose(ps[:, dc * D + oc * P:dc * D + (oc + 1) * P],
                                                   w[:, oc, dc * P:(dc + 1) * P], ident[:])
                last.then_inc(prep_pe, 1)
            for dc in range(DC):
                for b in range(B):
                    last = nc.tensor.transpose(ps_x[dc][:, b * KEYS:(b + 1) * KEYS], ctx_in[:, b, dc * P:(dc + 1) * P],
                                               ident[0:KEYS, 0:KEYS])
            last.then_inc(prep_pe, 1)
            pe.wait_ge(misc_loaded, 80)
            pe.wait_ge(consts_ready, 2)
            for k in range(DC):
                last = mm(ps_l[:, 64:64 + E], mean_of[:], router_in[:, k], start=k == 0, stop=k == DC - 1)
            last.then_inc(prep_pe, 1)
            pe.wait_ge(prep_sb, 4)
            for oc in range(DC):
                for k in range(DC):
                    mm(ps_l[:, oc:oc + 1], w2_t[:, k, oc * P:(oc + 1) * P], b1_in[:, k:k + 1], start=k == 0,
                       stop=k == DC - 1)
            for oc, ps in enumerate((ps_s, ps_p)):
                for k in range(DC):
                    last = mm(ps[:, 0:KB], w1_t[:, k, oc * P:(oc + 1) * P], ctx_t[:, k], start=k == 0, stop=k == DC - 1)
            last.then_inc(prep_pe, 1)
            pe.wait_ge(prep_sb, 6)
            for oc in range(DC):
                for k in range(DC):
                    last = mm(ps_q[oc][:, 0:KB], w2_t[:, k, oc * P:(oc + 1) * P], h_t[:, k], start=k == 0, stop=k == DC - 1)
            last.then_inc(prep_pe, 1)
            pe.wait_ge(prep_sb, 8)
            pe.wait_ge(prep_dve, 2)
            for k in range(DC):
                last = mm(ps_o[:].rearrange("p a d -> p (a d)")[:, 0:KB], bq_wide[:, k], kp_t[:, k], start=k == 0,
                          stop=k == DC - 1)
            last.then_inc(prep_pe, 1)
            for oc in range(DC):
                for k in range(DC):
                    last = mm(ps_x[oc][:, 0:KB], w2_in[:, k, oc * P:(oc + 1) * P], kp_t[:, k], start=k == 0, stop=k == DC - 1)
            last.then_inc(prep_pe, 1)
            pe.wait_ge(prep_sb, 10)
            for oc, ps in enumerate((ps_s, ps_p)):
                for k in range(DC):
                    last = mm(ps[:, 0:KB], w1_in[:, k, oc * P:(oc + 1) * P], u_t[:, k], start=k == 0, stop=k == DC - 1)
            last.then_inc(prep_pe, 1)

            def transpose_q(g):
                pe.wait_ge(q_ready, g + 1)
                if g:
                    pe.wait_ge(qt_ready, g)
                for k in range(DC):
                    for b in range(B):
                        last = nc.tensor.transpose(ps_q[k][:, b * P:(b + 1) * P], q[:, b, k * P:(k + 1) * P], ident[:])
                last.then_inc(qt_psum, 1)

            def transpose_probs(g):
                pe.wait_ge(probs_ready, g + 1)
                if g:
                    pe.wait_ge(pt_ready, g)
                for b in range(B):
                    last = nc.tensor.transpose(ps_p[0:KEYS, b * P:(b + 1) * P], probs[:, g % 2, b], ident[:])
                last.then_inc(pt_psum, 1)

            def transpose_x1(g):
                pe.wait_ge(x1_ready, 2 * (g + 1))
                if g:
                    pe.wait_ge(x1t_ready, g)
                for k in range(DC):
                    for b in range(B):
                        last = nc.tensor.transpose(ps_x[k][:, b * P:(b + 1) * P], x_row[:, g % 2, b, k * P:(k + 1) * P],
                                                   ident[:])
                last.then_inc(x1t_psum, 1)

            def scores(g):
                pe.wait_ge(qt_ready, g + 1)
                if g:
                    pe.wait_ge(masked_ready, g)
                for b in range(B):
                    for k in range(DC):
                        last = mm(ps_s[:, b * KEYS:(b + 1) * KEYS], q_t[:, k, b * P:(b + 1) * P],
                                  keys_t[:, k, b * KEYS:(b + 1) * KEYS], start=k == 0, stop=k == DC - 1)
                last.then_inc(scores_psum, 1)

            def attend(g, half):
                if half == 0:
                    pe.wait_ge(pt_ready, g + 1)
                if g or half:
                    pe.wait_ge(x1_ready, 2 * g + half)
                for b in range(2 * half, 2 * half + 2):
                    last = mm(ps_o[:, b % 2], probs_t[:, b * P:(b + 1) * P], values[:, b], start=True, stop=True)
                last.then_inc(attn_psum, 1)

            def route_logits(g):
                pe.wait_ge(x1t_ready, g + 1)
                if g:
                    pe.wait_ge(logits_ready, g)
                for b in range(B):
                    for k in range(DC):
                        last = mm(ps_l[:, b * E:(b + 1) * E], x1_t[:, k, b * P:(b + 1) * P], router_c[:, k],
                                  start=k == 0, stop=k == DC - 1)
                last.then_inc(logits_psum, 1)

            pe.wait_ge(prep_sb, 12)
            pe.wait_ge(prep_dve, 3)
            for i in range(1, NG + 3):
                if i - 1 < NG:
                    transpose_q(i - 1)
                if 0 <= i - 2 < NG:
                    transpose_probs(i - 2)
                if 0 <= i - 3 < NG:
                    transpose_x1(i - 3)
                if i - 1 < NG:
                    scores(i - 1)
                if 0 <= i - 2 < NG:
                    attend(i - 2, 0)
                if 0 <= i - 3 < NG:
                    route_logits(i - 3)
                if 0 <= i - 2 < NG:
                    attend(i - 2, 1)

            pe.wait_ge(onehot_ready, 1)
            pe.wait_ge(consts_ready, 3)
            hot = onehot[:].rearrange("p e t -> p (e t)")
            mm(ps_q[0][:, 0:E * NT], before[:], hot, start=True, stop=True)
            mm(ps_q[1][:, 0:E * NT], ones[:], hot, start=True, stop=True).then_inc(ranks_psum, 1)
            for n in range(NB):
                pe.wait_ge(slot_hot_ready, n + 1)
                pe.wait_ge(tile_hot_ready, n + 1)
                for t in range(n * HOT, (n + 1) * HOT):
                    last = mm(ps_s[:, 0:2 * COLS], slot_hot[:, t % 8], tile_hot[:, t % 8], start=t == 0, stop=t == NT - 1)
                last.then_inc(lists_step, 1)

            pe.wait_ge(lists_ready, 2)
            last_tile = pe.value_load(last_sorted[0:1, 0:1], min_val=E * MIN_TILES - 1, max_val=MAXT - 1)
            total = pe.snap(last_tile + 1)

            def transpose_x(t):
                pe.wait_ge(xnorm_ready, t + 1)
                if not (isinstance(t, int) and t == 0):
                    pe.wait_ge(xlo_ready, t)
                for k in range(DC):
                    last = nc.tensor.transpose(px[:, k * P:(k + 1) * P], x_norm[:, k * P:(k + 1) * P], ident[:])
                last.then_inc(xt_psum, 1)

            def up(t, j, slot):
                if j == 0:
                    pe.wait_ge(xlo_ready, t + 1)
                if not (isinstance(t, int) and t == 0):
                    pe.wait_ge(hidden_ready[j], t)
                n = 0
                for k in range(DC):
                    for xt, ws in ((xt_hi, (w_hi, w_lo)), (xt_lo, (w_hi,))):
                        for w in ws:
                            for ps, col in ((pa[j], j * HALF), (pg[j], F + j * HALF)):
                                last = mm(ps[:], xt[:, k], w[:, bass.ds(slot + (k * PW + col), HALF)], start=n == 0,
                                          stop=n == 3 * DC - 1)
                            n += 1
                last.then_inc(up_psum[j], 1)

            def transpose_h(t, j, start=False):
                pe.wait_ge(hidden_ready[j], t + 1)
                if j == 0 and not start:
                    pe.wait_ge(hlo_ready[0], t)
                for c in range(HC):
                    last = nc.tensor.transpose(ph[j][:, c * P:(c + 1) * P], hidden[:, j, c * P:(c + 1) * P], ident[:])
                last.then_inc(ht_psum[j], 1)

            def down(t, j, slot):
                pe.wait_ge(hlo_ready[j], t + 1)
                if j == 0:
                    pe.wait_ge(out_ready, t + 1)
                n = 0
                for c in range(HC):
                    for ht, ws in ((ht_hi, (w_hi, w_lo)), (ht_lo, (w_hi,))):
                        for w in ws:
                            last = mm(py[:, 0:D], ht[:, j, c * P:(c + 1) * P],
                                      w[:, bass.ds(slot + (DC * PW + (j * HC + c) * D), D)],
                                      start=j == 0 and n == 0, stop=j == 1 and n == 3 * HC - 1)
                            n += 1
                last.then_inc(down_psum[j], 1)

            transpose_x(0)
            pe.wait_ge(w_ready, PIECES)
            up(0, 0, 0)
            up(0, 1, 0)
            transpose_x(1)
            transpose_h(0, 0, start=True)
            with pe.Fori(1, total) as t:
                expert = pe.value_load(tile_expert[0:1, bass.ds(t, 1)], min_val=0, max_val=E - 1)
                slot = pe.snap((expert & 1) * EW)
                old = pe.value_load(tile_expert[0:1, bass.ds(t - 1, 1)], min_val=0, max_val=E - 1)
                old_slot = pe.snap((old & 1) * EW)
                pe.wait_ge(w_ready, expert * PIECES + PIECES)
                up(t, 0, slot)
                transpose_h(t - 1, 1)
                up(t, 1, slot)
                transpose_x(t + 1)
                transpose_h(t, 0)
                down(t - 1, 0, old_slot)
                down(t - 1, 1, old_slot)
            old = pe.value_load(tile_expert[0:1, bass.ds(last_tile, 1)], min_val=0, max_val=E - 1)
            old_slot = pe.snap((old & 1) * EW)
            transpose_h(last_tile, 1)
            down(last_tile, 0, old_slot)
            down(last_tile, 1, old_slot)


_INS = ['x', 'ctx_1024', 'fside_1xSxS2_0', 'g_xattn', 'g_ffn', 'L0_xattn_W1', 'L0_xattn_b1', 'L0_xattn_W2',
        'L0_xattn_b2', 'L0_ffn_router_w', 'L0_ffn_router_b', 'L0_ffn_w1', 'L0_ffn_w2']


def kernel(**inputs):
    import numpy as np
    import concourse.bacc as bacc
    from concourse.bass_utils import run_bass_kernel_spmd

    nc = bacc.Bacc("TRN2", target_bir_lowering=False, num_devices=1)
    arrays, args = {}, []
    for name in _INS:
        a = np.ascontiguousarray(inputs[name])
        arrays[f"in_{name}"] = a
        args.append(nc.dram_tensor(f"in_{name}", a.shape, mybir.dt.from_np(a.dtype), kind="ExternalInput").ap())
    x = inputs["x"]
    args.append(nc.dram_tensor("out_0", x.shape, mybir.dt.from_np(np.dtype("float32")), kind="ExternalOutput").ap())
    flamingo_block(nc, *args)
    r = run_bass_kernel_spmd(nc, [arrays], core_ids=[0])
    return r.results[0]["out_0"]
```

```python
from contextlib import ExitStack

import concourse.bass as bass
from concourse import mybir

FP32 = mybir.dt.float32
FP32R = mybir.dt.float32r
I32 = mybir.dt.int32
ALU = mybir.AluOpType
ACT = mybir.ActivationFunctionType
AX = mybir.AxisListType

P = 128


def flamingo_block(nc, x, ctx_kv, mask, g_xattn, g_ffn, w1, b1, w2, b2, router_w, router_b, e_w1, e_w2, out):
    B, S, D = x.shape
    KEYS = ctx_kv.shape[1]
    E, _, F2 = e_w1.shape
    F = F2 // 2
    DC = D // P
    NG = S // P
    N = B * S
    NT = N // P
    KB = B * KEYS
    EPS = 1e-5
    SCALE = float(D) ** -0.5
    ROW = D + 2
    MIN_TILES = 3
    PIECES = 3
    PW = F2
    EW = PIECES * PW
    MAXT = NT + MIN_TILES * (E - 1)
    COLS = MAXT + 2
    HALF = 512
    HC = HALF // P
    HOT = 8
    RES = 4
    XR = 4
    assert DC == 2 and F == 2 * HALF and (F // P) * D == PW and D * F2 == DC * P * PW

    x_groups = x.rearrange("b (s p) d -> s p b d", p=P)
    mask_groups = mask.rearrange("a (s p) k -> p (a s) k", p=P)
    out_rows = out.rearrange("b s d -> (b s) d")
    rows = nc.dram_tensor("residual_rows", (N, ROW), FP32).ap()
    rows_groups = rows.rearrange("(b s p) c -> s p b c", b=B, p=P)
    e_w1_pieces = e_w1.rearrange("e (k p) n -> (e k) p n", p=P)
    e_w2_pieces = e_w2.rearrange("e (c p) n -> e p c n", p=P)

    with ExitStack() as top:
        def buffers(stack, make):
            return lambda name, shape, dt=FP32: stack.enter_context(make(name, shape, dt))

        sb = buffers(top, nc.sbuf_tensor)

        def sem(name):
            return top.enter_context(nc.semaphore(name))

        w_hi = sb("w_hi", [P, 2 * EW], FP32R)
        w_lo = sb("w_lo", [P, 2 * EW], FP32R)
        staging = sb("staging", [P, PIECES * PW])
        ident = sb("ident", [P, P])
        col_of_tile = sb("col_of_tile", [P, COLS])
        tanh_g = sb("tanh_g", [P, 2])
        idx_gather = sb("idx_gather", [P, COLS], I32)
        idx_scatter = sb("idx_scatter", [P, COLS], I32)
        gate_sorted = sb("gate_sorted", [P, COLS])
        tables = sb("tables", [4, P], I32)
        tile_expert, tile_first, tile_piece, last_sorted = (tables[r:r + 1, :] for r in range(4))

        part1 = ExitStack()
        sb1 = buffers(part1, nc.sbuf_tensor)
        ps1 = buffers(part1, nc.psum_tensor)
        x_in = sb1("x_in", [P, XR, B, D])
        x_row = sb1("x_row", [P, 2, B, ROW])
        mask_in = sb1("mask_in", [P, NG, KEYS])
        mask_c = sb1("mask_c", [P, 2, B, KEYS])
        bias_c = sb1("bias_c", [P, KB])
        keys_t = sb1("keys_t", [P, DC, KB])
        values = sb1("values", [KEYS, B, D])
        router_c = sb1("router_c", [P, DC, E])
        router_b_all = sb1("router_b_all", [P, E])
        bn1 = sb1("bn1", [P, 2, B, 6])
        mv1 = sb1("mv1", [P, 2, B, 2])
        rstd1 = sb1("rstd1", [P, 2, B])
        bn2 = sb1("bn2", [P, 2, B, 6])
        mv2 = sb1("mv2", [P, 2, B, 2])
        rstd2 = sb1("rstd2", [P, NG, B])
        var_eps = sb1("var_eps", [P, 2, 2, B])
        minus_half = sb1("minus_half", [P, B])
        x_t = sb1("x_t", [P, DC, B * P])
        masked = sb1("masked", [P, B, KEYS])
        neg_max = sb1("neg_max", [P, 2, B])
        probs = sb1("probs", [P, 2, B, KEYS])
        prob_sum = sb1("prob_sum", [P, 2, B])
        prob_inv = sb1("prob_inv", [P, 2, B])
        probs_t = sb1("probs_t", [KEYS, B * P])
        x1_t = sb1("x1_t", [P, DC, B * P])
        logits = sb1("logits", [P, NT, E])

        prep = ExitStack()
        sb0 = buffers(prep, nc.sbuf_tensor)
        ctx_in = sb0("ctx_in", [KEYS, B, D])
        w1_in = sb0("w1_in", [P, DC, D])
        w2_in = sb0("w2_in", [P, DC, D])
        w1_mean = sb0("w1_mean", [P, 2, DC])
        w1_c = sb0("w1_c", [P, DC, D])
        w2_t = sb0("w2_t", [P, DC, D])
        ctx_t = sb0("ctx_t", [P, DC, KB])
        m_t = sb0("m_t", [P, DC, D])
        m_c = sb0("m_c", [P, DC, D])
        b1_in = sb0("b1_in", [P, DC])
        b2_in = sb0("b2_in", [P, DC])
        bq = sb0("bq", [P, DC])
        bq_wide = sb0("bq_wide", [P, DC, P])
        router_in = sb0("router_in", [P, DC, E])
        mean_of = sb0("mean_of", [P, P])
        gates_in = sb0("gates_in", [P, 2])
        kp_t = sb0("kp_t", [P, DC, KB])
        prep.close()

        sbr = buffers(part1, nc.sbuf_tensor)
        before = sbr("before", [P, P])
        ones = sbr("ones", [P, P])
        ones_wide = sbr("ones_wide", [P, E * NT])
        slot_iota = sbr("slot_iota", [P, P])
        expert_m8 = sbr("expert_m8", [P, E])
        token_mN = sbr("token_mN", [P, NT])
        onehot = sbr("onehot", [P, E, NT])
        work_a = sbr("work_a", [P, NT, E])
        work_b = sbr("work_b", [P, NT, E])
        best = sbr("best", [P, NT])
        first = sbr("first", [P, NT])
        gate = sbr("gate", [P, NT])
        cum = sbr("cum", [P, E * NT])
        starts = sbr("starts", [P, E + 1])
        counts_i = sbr("counts_i", [P, E], I32)
        tiles_i = sbr("tiles_i", [P, E], I32)
        tiles_f = sbr("tiles_f", [P, E])
        bounds = sbr("bounds", [P, E + 1])
        shift = sbr("shift", [P, E])
        pos_i = sbr("pos_i", [P, 3, NT], I32)
        pos_f = sbr("pos_f", [P, 2, NT])
        slot_hot = x_in[:].rearrange("p r b d -> p (r b d)").rearrange("p (t s) -> p t s", s=P)
        tile_eq = sbr("tile_eq", [P, HOT, COLS])
        tile_hot = sbr("tile_hot", [P, NT, 2, COLS])
        part_iota = sbr("part_iota", [P, 1])
        tab_w = sbr("tab_w", [P, 2, E])
        tab_k = sbr("tab_k", [P, 3])
        tab = sbr("tab", [P, 4])

        ps_q = [ps1(f"ps_q{k}", [P, B * P]) for k in range(DC)]
        ps_x = [ps1(f"ps_x{k}", [P, B * P]) for k in range(DC)]
        ps_s = ps1("ps_s", [P, 512])
        ps_p = ps1("ps_p", [P, 512])
        ps_o = ps1("ps_o", [P, 2, D])
        ps_l = ps1("ps_l", [P, 512])
        part1.close()

        part2 = ExitStack()
        sb2 = buffers(part2, nc.sbuf_tensor)
        ps2 = buffers(part2, nc.psum_tensor)
        idx_now = sb2("idx_now", [P, 2], I32)
        x_sorted = sb2("x_sorted", [P, ROW])
        x_norm = sb2("x_norm", [P, D])
        residual = sb2("residual", [P, RES * D])
        xt_hi = sb2("xt_hi", [P, DC, P], FP32R)
        xt_lo = sb2("xt_lo", [P, DC, P], FP32R)
        silu = sb2("silu", [P, 2, HALF])
        hidden = sb2("hidden", [P, 2, HALF])
        ht_hi = sb2("ht_hi", [P, 2, HALF], FP32R)
        ht_lo = sb2("ht_lo", [P, 2, HALF], FP32R)
        out_tile = sb2("out_tile", [P, D])
        pa = [ps2(f"pa{j}", [P, HALF]) for j in range(2)]
        pg = [ps2(f"pg{j}", [P, HALF]) for j in range(2)]
        ph = [ps2(f"ph{j}", [P, HALF]) for j in range(2)]
        py = ps2("py", [P, HALF])
        px = ps2("px", [P, HALF])
        part2.close()

        proj_loaded = sem("proj_loaded")
        misc_loaded = sem("misc_loaded")
        x_loaded = [sem(f"x_loaded{i}") for i in range(XR)]
        rows_stored = [sem(f"rows_stored{i}") for i in range(2)]
        piece_loaded = sem("piece_loaded")
        consts_ready = sem("consts_ready")
        tanh_ready = sem("tanh_ready")
        prep_pe = sem("prep_pe")
        prep_sb = sem("prep_sb")
        prep_dve = sem("prep_dve")
        bn1_ready = sem("bn1_ready")
        mv1_ready = sem("mv1_ready")
        pool_step = sem("pool_step")
        rstd1_ready = sem("rstd1_ready")
        mt_ready = sem("mt_ready")
        bias_ready = sem("bias_ready")
        tab_ready = sem("tab_ready")
        tab_psum = sem("tab_psum")
        rstd2_ready = sem("rstd2_ready")
        mask_c_ready = sem("mask_c_ready")
        xt1_psum = sem("xt1_psum")
        xt1_ready = sem("xt1_ready")
        scores_psum = sem("scores_psum")
        masked_ready = sem("masked_ready")
        max_ready = sem("max_ready")
        probs_ready = sem("probs_ready")
        pt_psum = sem("pt_psum")
        pt_ready = sem("pt_ready")
        inv_ready = sem("inv_ready")
        attn_psum = sem("attn_psum")
        x1_ready = sem("x1_ready")
        bn2_ready = sem("bn2_ready")
        mv2_ready = sem("mv2_ready")
        x1t_psum = sem("x1t_psum")
        x1t_ready = sem("x1t_ready")
        logits_psum = sem("logits_psum")
        logits_ready = sem("logits_ready")
        route_step = sem("route_step")
        route_pool = sem("route_pool")
        centered = sem("centered")
        gate_exp = sem("gate_exp")
        onehot_ready = sem("onehot_ready")
        ranks_psum = sem("ranks_psum")
        pos_ready = sem("pos_ready")
        gate_ready = sem("gate_ready")
        act_distance = sem("act_distance")
        act_slot_hot = sem("act_slot_hot")
        pool_slot_hot = sem("pool_slot_hot")
        tile_hot_ready = sem("tile_hot_ready")
        lists_step = sem("lists_step")
        lists_ready = sem("lists_ready")
        tables_ready = sem("tables_ready")
        w_hi_ready = sem("w_hi_ready")
        w_ready = sem("w_ready")
        idx_now_ready = sem("idx_now_ready")
        gathered = sem("gathered")
        res_ready = sem("res_ready")
        xnorm_ready = sem("xnorm_ready")
        xt_psum = sem("xt_psum")
        xhi_ready = sem("xhi_ready")
        xlo_ready = sem("xlo_ready")
        up_psum = [sem(f"up_psum{j}") for j in range(2)]
        silu_ready = [sem(f"silu_ready{j}") for j in range(2)]
        hidden_ready = [sem(f"hidden_ready{j}") for j in range(2)]
        ht_psum = [sem(f"ht_psum{j}") for j in range(2)]
        hhi_ready = [sem(f"hhi_ready{j}") for j in range(2)]
        hlo_ready = [sem(f"hlo_ready{j}") for j in range(2)]
        down_psum = [sem(f"down_psum{j}") for j in range(2)]
        out_ready = sem("out_ready")
        scattered = sem("scattered")

        NB = NT // HOT
        W_CHUNK = PW // 2
        N_CHUNK = PIECES * PW // W_CHUNK

        block = top.enter_context(nc.Block())

        @block.sync
        def _(sp):
            sp.dma_start(ctx_in[:], ctx_kv.rearrange("b k d -> k b d")).then_inc(proj_loaded, 16)
            sp.dma_start(w1_in[:], w1.rearrange("(c p) d -> p c d", p=P)).then_inc(proj_loaded, 16)
            sp.dma_start(w2_in[:], w2.rearrange("(c p) d -> p c d", p=P)).then_inc(proj_loaded, 16)
            with nc.allow_non_contiguous_dma(reason="small vectors"):
                sp.dma_start(b1_in[:], b1.rearrange("(c p) -> p c", p=P)).then_inc(proj_loaded, 16)
                sp.dma_start(b2_in[:], b2.rearrange("(c p) -> p c", p=P)).then_inc(proj_loaded, 16)
            sp.dma_start(x_in[:, 0], x_groups[0]).then_inc(x_loaded[0], 16)
            sp.dma_start(gates_in[:, 0:1], g_xattn.partition_broadcast(P)).then_inc(misc_loaded, 16)
            sp.dma_start(gates_in[:, 1:2], g_ffn.partition_broadcast(P)).then_inc(misc_loaded, 16)
            sp.dma_start(mask_in[:], mask_groups).then_inc(misc_loaded, 16)
            sp.dma_start(router_in[:], router_w.rearrange("(c p) e -> p c e", p=P)).then_inc(misc_loaded, 16)
            sp.dma_start(router_b_all[:], router_b.partition_broadcast(P)).then_inc(misc_loaded, 16)
            for g in range(1, XR):
                sp.dma_start(x_in[:, g], x_groups[g]).then_inc(x_loaded[g], 16)
            for k in range(DC):
                if k:
                    sp.wait_ge(piece_loaded, 16 * k)
                sp.dma_start(staging[:, k * PW:(k + 1) * PW], e_w1_pieces[k]).then_inc(piece_loaded, 16)
            sp.wait_ge(piece_loaded, 16 * DC)
            sp.dma_start(staging[:, DC * PW:EW].rearrange("p (c n) -> p c n", n=D), e_w2_pieces[0]).then_inc(piece_loaded, 16)
            for g in range(NG):
                if g + XR < NG:
                    sp.wait_ge(x1_ready, 2 * (g + 1))
                    sp.dma_start(x_in[:, g % XR], x_groups[g + XR]).then_inc(x_loaded[g % XR], 16)
                sp.wait_ge(rstd2_ready, g + 1)
                sp.dma_start(rows_groups[g], x_row[:, g % 2]).then_inc(rows_stored[g % 2], 16)
            for p in range(PIECES, E * PIECES):
                e, k = divmod(p, PIECES)
                sp.wait_ge(w_ready, p + 1 - PIECES)
                sp.wait_ge(piece_loaded, 16 * p)
                at = staging[:, k * PW:(k + 1) * PW]
                if k < DC:
                    sp.dma_start(at, e_w1_pieces[e * DC + k]).then_inc(piece_loaded, 16)
                else:
                    sp.dma_start(at.rearrange("p (c n) -> p c n", n=D), e_w2_pieces[e]).then_inc(piece_loaded, 16)

        @block.gpsimd
        def _(pool):
            step = [0]

            def link(instruction):
                step[0] += 1
                instruction.then_inc(pool_step, 1)
                pool.wait_ge(pool_step, step[0])

            link(nc.gpsimd.memset(ident[:], 0.0))
            nc.gpsimd.affine_select(out=ident[:], in_=ident[:], compare_op=ALU.not_equal, fill=1.0, base=0,
                                    pattern=[[-1, P]], channel_multiplier=1).then_inc(consts_ready, 1)
            nc.gpsimd.memset(mean_of[:], 1.0 / D)
            nc.gpsimd.memset(minus_half[:], -0.5).then_inc(consts_ready, 1)

            def norm1(g):
                r = g % 2
                pool.wait_ge(mv1_ready, g + 1)
                if g >= 2:
                    pool.wait_ge(masked_ready, g - 1)
                link(nc.gpsimd.tensor_scalar(var_eps[:, 0, r], mv1[:, r, :, 1], EPS, None, ALU.add))
                nc.gpsimd.tensor_tensor(out=rstd1[:, r], in0=var_eps[:, 0, r], in1=minus_half[:],
                                        op=ALU.pow).then_inc(rstd1_ready, 1)

            def mask1(g):
                if g == 0:
                    pool.wait_ge(misc_loaded, 80)
                    pool.wait_ge(bias_ready, 1)
                if g >= 2:
                    pool.wait_ge(masked_ready, g - 1)
                nc.gpsimd.tensor_tensor(out=mask_c[:, g % 2], in0=bias_c[:].rearrange("p (b k) -> p b k", b=B),
                                        in1=mask_in[:, g:g + 1, :].to_broadcast([P, B, KEYS]),
                                        op=ALU.add).then_inc(mask_c_ready, 1)

            def norm2(g):
                r = g % 2
                pool.wait_ge(mv2_ready, g + 1)
                link(nc.gpsimd.tensor_scalar(var_eps[:, 1, r], mv2[:, r, :, 1], EPS, None, ALU.add))
                link(nc.gpsimd.tensor_tensor(out=rstd2[:, g], in0=var_eps[:, 1, r], in1=minus_half[:], op=ALU.pow))
                nc.gpsimd.tensor_copy(x_row[:, r, :, D + 1], rstd2[:, g])
                nc.gpsimd.tensor_tensor(out=x_row[:, r, :, D], in0=mv2[:, r, :, 0], in1=rstd2[:, g],
                                        op=ALU.mult).then_inc(rstd2_ready, 1)

            def low0(c):
                pool.wait_ge(w_hi_ready, c + 1)
                at = slice(c * W_CHUNK, (c + 1) * W_CHUNK)
                lo = nc.gpsimd.tensor_tensor(out=w_lo[:, at], in0=staging[:, at], in1=w_hi[:, at].bitcast(FP32),
                                             op=ALU.subtract)
                if c % 2:
                    lo.then_inc(w_ready, 1)

            norm1(0)
            for i in range(1, NG + 2):
                if i - 1 < NG:
                    mask1(i - 1)
                if i < NG:
                    norm1(i)
                if 0 <= i - 2 < NG:
                    norm2(i - 2)
                if 0 <= i - 2 < N_CHUNK:
                    low0(i - 2)

            rstep = [0]

            def rlink(instruction):
                rstep[0] += 1
                instruction.then_inc(route_pool, 1)
                pool.wait_ge(route_pool, rstep[0])

            rlink(nc.gpsimd.memset(before[:], 1.0))
            nc.gpsimd.affine_select(out=before[:], in_=before[:], compare_op=ALU.is_gt, fill=0.0, base=0,
                                    pattern=[[1, P]], channel_multiplier=-1)
            nc.gpsimd.memset(ones[:], 1.0)
            nc.gpsimd.memset(ones_wide[:], 1.0)
            nc.gpsimd.iota(part_iota[:], [[0, 1]], base=0, channel_multiplier=1, allow_small_or_imprecise_dtypes=True)
            nc.gpsimd.iota(slot_iota[:], [[1, P]], base=0, channel_multiplier=0, allow_small_or_imprecise_dtypes=True)
            nc.gpsimd.iota(expert_m8[:], [[1, E]], base=-E, channel_multiplier=0, allow_small_or_imprecise_dtypes=True)
            nc.gpsimd.iota(token_mN[:].rearrange("p (g b) -> p g b", b=B), [[P, NG], [S, B]], base=-N,
                           channel_multiplier=1, allow_small_or_imprecise_dtypes=True)
            nc.gpsimd.iota(col_of_tile[:], [[1, COLS]], base=0, channel_multiplier=0,
                           allow_small_or_imprecise_dtypes=True).then_inc(consts_ready, 1)
            pool.wait_ge(pos_ready, 1)
            pool.wait_ge(consts_ready, 3)
            for t in range((NB - 1) * HOT, NT):
                last = nc.gpsimd.tensor_scalar(slot_hot[:, t], slot_iota[:], pos_f[:, 1, t:t + 1], None, ALU.is_equal)
            last.then_inc(pool_slot_hot, 1)

            pool.wait_ge(lists_ready, 2)
            pool.wait_ge(tables_ready, 1)
            for i in range(2):
                pool.wait_ge(rows_stored[i], 16 * (NG // 2))
            last_tile = pool.value_load(last_sorted[:, 0:1], min_val=E * MIN_TILES - 1, max_val=MAXT - 1)
            total = pool.snap(last_tile + 1)

            def last_row(t):
                return N - 1 if isinstance(t, int) else pool.snap((t >> 6) + (N - 1))

            def gather(t, now):
                nc.gpsimd.tensor_copy(idx_now[:, 0:1], idx_gather[:, bass.ds(t, 1)]).then_inc(idx_now_ready, 1)
                pool.wait_ge(idx_now_ready, now + 1)
                pool.indirect_dma_start(x_sorted[:], None, rows, bass.IndirectOffsetOnAxis(ap=idx_now[:, 0:1], axis=0),
                                        bounds_check=last_row(t), oob_is_err=False).then_inc(gathered, 16)

            def scatter(t, now):
                pool.wait_ge(out_ready, t + 2)
                nc.gpsimd.tensor_copy(idx_now[:, 1:2], idx_scatter[:, bass.ds(t, 1)]).then_inc(idx_now_ready, 1)
                pool.wait_ge(idx_now_ready, now + 1)
                pool.indirect_dma_start(out_rows, bass.IndirectOffsetOnAxis(ap=idx_now[:, 1:2], axis=0), out_tile[:],
                                        None, bounds_check=last_row(t), oob_is_err=False).then_inc(scattered, 16)

            def low_part(t):
                piece = pool.value_load(tile_piece[:, bass.ds(t, 1)], min_val=0, max_val=E * PIECES - 1)
                with pool.If(piece > 0):
                    src = pool.snap((piece % PIECES) * PW)
                    dst = pool.snap(((piece // PIECES) & 1) * EW + src)
                    pool.wait_ge(w_hi_ready, piece + (N_CHUNK - PIECES + 1))
                    nc.gpsimd.tensor_tensor(out=w_lo[:, bass.ds(dst, PW)], in0=staging[:, bass.ds(src, PW)],
                                            in1=w_hi[:, bass.ds(dst, PW)].bitcast(FP32), op=ALU.subtract).then_inc(w_ready, 1)

            for t in range(3):
                if t:
                    pool.wait_ge(xnorm_ready, t)
                    pool.wait_ge(res_ready, t)
                gather(t, t)
            low_part(0)
            with pool.Fori(1, total) as t:
                pool.wait_ge(xnorm_ready, t + 2)
                pool.wait_ge(res_ready, t + 2)
                gather(t + 2, t * 2 + 1)
                scatter(t - 1, t * 2 + 2)
                low_part(t)
            scatter(last_tile, total * 2 + 1)
            pool.wait_ge(gathered, total * 16 + 32)
            pool.wait_ge(scattered, total * 16)

        @block.scalar
        def _(act):
            act.wait_ge(misc_loaded, 80)
            nc.scalar.activation(tanh_g[:], gates_in[:], ACT.Tanh).then_inc(tanh_ready, 1)
            act.wait_ge(prep_pe, 1)
            nc.scalar.copy(w2_t[:], ps_q[0][:].rearrange("p (c d) -> p c d", c=DC)).then_inc(prep_sb, 1)
            act.wait_ge(prep_pe, 2)
            nc.scalar.copy(ctx_t[:, 0], ps_x[0][:, 0:KB]).then_inc(prep_sb, 1)
            act.wait_ge(prep_pe, 4)
            nc.scalar.copy(m_t[:], ps_p[:].rearrange("p (c d) -> p c d", c=DC)).then_inc(mt_ready, 1)
            act.wait_ge(prep_pe, 6)
            act.wait_ge(prep_dve, 4)
            nc.scalar.activation(kp_t[:, 0], ps_q[0][:, 0:KB], ACT.Identity, bias=bq[:, 0:1]).then_inc(prep_sb, 1)
            act.wait_ge(prep_pe, 8)
            nc.scalar.mul(keys_t[:, 0], ps_x[0][:, 0:KB], SCALE).then_inc(prep_sb, 1)

            def high0(c):
                if c % 2 == 0:
                    act.wait_ge(piece_loaded, 16 * (c // 2 + 1))
                at = slice(c * W_CHUNK, (c + 1) * W_CHUNK)
                nc.scalar.copy(w_hi[:, at], staging[:, at]).then_inc(w_hi_ready, 1)

            def copy_xt(g):
                act.wait_ge(xt1_psum, g + 1)
                if g:
                    act.wait_ge(scores_psum, g)
                for k in range(DC):
                    last = nc.scalar.copy(x_t[:, k], ps_q[k][:])
                last.then_inc(xt1_ready, 1)

            def copy_pt(g):
                act.wait_ge(pt_psum, g + 1)
                if g:
                    act.wait_ge(attn_psum, 2 * g)
                nc.scalar.copy(probs_t[:], ps_p[0:KEYS, :]).then_inc(pt_ready, 1)

            def copy_x1t(g):
                act.wait_ge(x1t_psum, g + 1)
                if g:
                    act.wait_ge(logits_psum, g)
                for k in range(DC):
                    last = nc.scalar.copy(x1_t[:, k], ps_x[k][:])
                last.then_inc(x1t_ready, 1)

            def softmax(g):
                r = g % 2
                act.wait_ge(max_ready, g + 1)
                if g >= 2:
                    act.wait_ge(pt_psum, g - 1)
                    act.wait_ge(inv_ready, g - 1)
                for b in range(B):
                    last = nc.scalar.activation(probs[:, r, b], masked[:, b], ACT.Exp, bias=neg_max[:, r, b:b + 1],
                                                accum_out=prob_sum[:, r, b:b + 1])
                last.then_inc(probs_ready, 1)

            for i in range(1, NG + 3):
                if i - 1 < NG:
                    copy_xt(i - 1)
                if 0 <= i - 2 < NG:
                    copy_pt(i - 2)
                if 0 <= i - 3 < NG:
                    copy_x1t(i - 3)
                if i - 1 < NG:
                    softmax(i - 1)
                if i - 1 < N_CHUNK:
                    high0(i - 1)

            act.wait_ge(centered, 1)
            nc.scalar.activation(work_b[:], work_b[:], ACT.Exp).then_inc(gate_exp, 1)

            act.wait_ge(pos_ready, 1)
            act.wait_ge(consts_ready, 3)
            for n in range(1, NB - 1):
                for t in range(n * HOT, (n + 1) * HOT):
                    last = nc.scalar.activation(slot_hot[:, t], slot_iota[:], ACT.Abs, bias=pos_f[:, 1, t:t + 1], scale=-1.0)
                last.then_inc(act_distance, 1)
                act.wait_ge(act_distance, n)
                batch = slot_hot[:, n * HOT:(n + 1) * HOT]
                nc.scalar.activation(batch, batch, ACT.Relu, bias=ones[:, 0:1], scale=-1.0).then_inc(act_slot_hot, 1)
            act.wait_ge(tab_psum, 1)
            nc.scalar.copy(tables[:], ps_l[0:4, 0:P]).then_inc(tables_ready, 1)

            act.wait_ge(tables_ready, 1)
            last_tile = act.value_load(last_sorted[:, 0:1], min_val=E * MIN_TILES - 1, max_val=MAXT - 1)
            total = act.snap(last_tile + 1)

            def x_high(t):
                act.wait_ge(xt_psum, t + 1)
                nc.scalar.copy(xt_hi[:], px[:, 0:D].rearrange("p (k n) -> p k n", k=DC)).then_inc(xhi_ready, 1)

            def residual_copy(t):
                act.wait_ge(gathered, t * 16 + 16)
                act.wait_ge(gathered, t * 16 + 16)
                nc.scalar.copy(residual[:, bass.ds((t & (RES - 1)) * D, D)], x_sorted[:, 0:D]).then_inc(res_ready, 1)

            def gate_half(t, j, start):
                act.wait_ge(up_psum[j], t + 1)
                if not start:
                    act.wait_ge(hidden_ready[j], t)
                nc.scalar.activation(silu[:, j], pa[j][:], ACT.Silu).then_inc(silu_ready[j], 1)

            def h_high(t, j, start):
                act.wait_ge(ht_psum[j], t + 1)
                if not start:
                    act.wait_ge(down_psum[j], t + j)
                nc.scalar.copy(ht_hi[:, j], ph[j][:]).then_inc(hhi_ready[j], 1)

            residual_copy(0)
            x_high(0)

            def tile(t, start):
                gate_half(t, 0, start)
                residual_copy(t + 1)
                act.wait_ge(up_psum[1], t + 1)
                x_high(t + 1)
                gate_half(t, 1, start)
                piece = act.value_load(tile_piece[:, bass.ds(t, 1)], min_val=0, max_val=E * PIECES - 1)
                first = act.value_load(tile_first[:, bass.ds(t, 1)], min_val=0, max_val=MAXT)
                h_high(t, 0, start)
                with act.If(piece > 0):
                    slot = ((piece // PIECES) & 1) * EW
                    src = (piece % PIECES) * PW
                    act.wait_ge(down_psum[1], first + 1)
                    act.wait_ge(piece_loaded, (piece + 1) * 16)
                    act.wait_ge(piece_loaded, (piece + 1) * 16)
                    nc.scalar.copy(w_hi[:, bass.ds(slot + src, PW)], staging[:, bass.ds(src, PW)]).then_inc(w_hi_ready, 1)
                h_high(t, 1, start)

            tile(0, True)
            with act.Fori(1, total) as t:
                tile(t, False)

        @block.vector
        def _(dve):
            dve.wait_ge(proj_loaded, 80)
            nc.vector.tensor_reduce(w1_mean[:, 0], w1_in[:], AX.X, ALU.add).then_inc(prep_dve, 1)
            dve.wait_ge(prep_dve, 1)
            nc.vector.tensor_scalar(w1_mean[:, 1], w1_mean[:, 0], 1.0 / D, None, ALU.mult).then_inc(prep_dve, 1)
            dve.wait_ge(prep_dve, 2)
            nc.vector.tensor_tensor(out=w1_c[:], in0=w1_in[:], in1=w1_mean[:, 1].unsqueeze(2).to_broadcast([P, DC, D]),
                                    op=ALU.subtract).then_inc(prep_dve, 1)
            dve.wait_ge(prep_pe, 2)
            nc.vector.tensor_copy(ctx_t[:, 1], ps_x[1][:, 0:KB]).then_inc(prep_sb, 1)
            dve.wait_ge(tanh_ready, 1)
            nc.vector.tensor_scalar(values[:], ctx_in[:], tanh_g[0:KEYS, 0:1], None, ALU.mult)
            dve.wait_ge(prep_pe, 3)
            nc.vector.tensor_tensor(out=router_c[:], in0=router_in[:],
                                    in1=ps_o[:, 1, 0:E].unsqueeze(1).to_broadcast([P, DC, E]), op=ALU.subtract)
            dve.wait_ge(prep_pe, 4)
            nc.vector.tensor_tensor(out=bq[:], in0=ps_l[:, 0:DC], in1=b2_in[:], op=ALU.add).then_inc(prep_dve, 1)
            dve.wait_ge(prep_dve, 4)
            nc.vector.tensor_copy(bq_wide[:], bq[:].unsqueeze(2).to_broadcast([P, DC, P])).then_inc(prep_dve, 1)
            dve.wait_ge(prep_pe, 5)
            nc.vector.tensor_copy(m_c[:], ps_s[:].rearrange("p (c d) -> p c d", c=DC)).then_inc(prep_sb, 1)
            dve.wait_ge(prep_pe, 6)
            nc.vector.tensor_scalar(kp_t[:, 1], ps_q[1][:, 0:KB], bq[:, 1:2], None, ALU.add).then_inc(prep_sb, 1)

            def last_of_preparation():
                dve.wait_ge(prep_pe, 7)
                nc.vector.tensor_scalar(bias_c[:], ps_o[:].rearrange("p a d -> p (a d)")[:, 0:KB], SCALE, None,
                                        ALU.mult).then_inc(bias_ready, 1)
                dve.wait_ge(prep_pe, 8)
                nc.vector.tensor_scalar(keys_t[:, 1], ps_x[1][:, 0:KB], SCALE, None, ALU.mult).then_inc(prep_sb, 1)

            def stats1(g):
                r = g % 2
                dve.wait_ge(x_loaded[g % XR], 16 * (g // XR + 1))
                for b in range(B):
                    last = nc.vector.bn_stats(bn1[:, r, b], x_in[:, g % XR, b])
                last.then_inc(bn1_ready, 1)
                dve.wait_ge(bn1_ready, g + 1)
                if g >= 2:
                    dve.wait_ge(rstd1_ready, g - 1)
                for b in range(B):
                    last = nc.vector.bn_aggr(mv1[:, r, b], bn1[:, r, b])
                last.then_inc(mv1_ready, 1)

            def mask_and_max(g):
                r = g % 2
                dve.wait_ge(scores_psum, g + 1)
                dve.wait_ge(mask_c_ready, g + 1)
                if g:
                    dve.wait_ge(probs_ready, g)
                dve.wait_ge(rstd1_ready, g + 1)
                for b in range(B):
                    last = nc.vector.scalar_tensor_tensor(out=masked[:, b], in0=ps_s[:, b * KEYS:(b + 1) * KEYS],
                                                          scalar=rstd1[:, r, b:b + 1], in1=mask_c[:, r, b],
                                                          op0=ALU.mult, op1=ALU.add)
                last.then_inc(masked_ready, 1)
                dve.wait_ge(masked_ready, g + 1)
                nc.vector.tensor_reduce(neg_max[:, r], masked[:], AX.X, ALU.max, negate=True).then_inc(max_ready, 1)

            def invert_sums(g):
                r = g % 2
                dve.wait_ge(probs_ready, g + 1)
                nc.vector.reciprocal(prob_inv[:, r], prob_sum[:, r]).then_inc(inv_ready, 1)
                dve.wait_ge(inv_ready, g + 1)

            def add_attention(g, half):
                r = g % 2
                dve.wait_ge(attn_psum, 2 * g + half + 1)
                if half == 0 and g >= 2:
                    dve.wait_ge(rows_stored[r], 16 * (g // 2))
                    dve.wait_ge(x1t_psum, g - 1)
                for b in range(2 * half, 2 * half + 2):
                    last = nc.vector.scalar_tensor_tensor(out=x_row[:, r, b, 0:D], in0=ps_o[:, b % 2],
                                                          scalar=prob_inv[:, r, b:b + 1], in1=x_in[:, g % XR, b],
                                                          op0=ALU.mult, op1=ALU.add)
                last.then_inc(x1_ready, 1)

            def stats2(g):
                r = g % 2
                dve.wait_ge(x1_ready, 2 * (g + 1))
                for b in range(B):
                    last = nc.vector.bn_stats(bn2[:, r, b], x_row[:, r, b, 0:D])
                last.then_inc(bn2_ready, 1)
                dve.wait_ge(bn2_ready, g + 1)
                if g >= 2:
                    dve.wait_ge(rstd2_ready, g - 1)
                for b in range(B):
                    last = nc.vector.bn_aggr(mv2[:, r, b], bn2[:, r, b])
                last.then_inc(mv2_ready, 1)

            def keep_logits(g):
                dve.wait_ge(logits_psum, g + 1)
                nc.vector.tensor_copy(logits[:, g * B:(g + 1) * B], ps_l[:, 0:B * E].rearrange("p (b e) -> p b e", b=B)
                                      ).then_inc(logits_ready, 1)

            stats1(0)
            last_of_preparation()
            for i in range(1, NG + 3):
                if i - 1 < NG:
                    mask_and_max(i - 1)
                if 0 <= i - 2 < NG:
                    invert_sums(i - 2)
                    add_attention(i - 2, 0)
                if i < NG:
                    stats1(i)
                if 0 <= i - 2 < NG:
                    add_attention(i - 2, 1)
                    stats2(i - 2)
                if 0 <= i - 3 < NG:
                    keep_logits(i - 3)

            step = [0]

            def link(instruction):
                step[0] += 1
                instruction.then_inc(route_step, 1)
                dve.wait_ge(route_step, step[0])

            def over_experts(v):
                return v.unsqueeze(2).to_broadcast([P, NT, E])

            def over_tiles(v):
                return v.unsqueeze(1).to_broadcast([P, NT, E])

            dve.wait_ge(logits_ready, NG)
            dve.wait_ge(rstd2_ready, NG)
            link(nc.vector.tensor_tensor(out=work_a[:], in0=logits[:], in1=over_experts(rstd2[:].rearrange("p g b -> p (g b)")),
                                         op=ALU.mult))
            link(nc.vector.tensor_tensor(out=logits[:], in0=work_a[:], in1=over_tiles(router_b_all[:]), op=ALU.add))
            link(nc.vector.tensor_reduce(best[:], logits[:], AX.X, ALU.max))
            nc.vector.tensor_tensor(out=work_b[:], in0=logits[:], in1=over_experts(best[:]), op=ALU.subtract).then_inc(centered, 1)
            link(nc.vector.tensor_tensor(out=work_a[:], in0=logits[:], in1=over_experts(best[:]), op=ALU.is_equal))
            dve.wait_ge(consts_ready, 3)
            link(nc.vector.tensor_tensor(out=work_a[:], in0=work_a[:], in1=over_tiles(expert_m8[:]), op=ALU.mult))
            link(nc.vector.tensor_reduce(first[:], work_a[:], AX.X, ALU.min))
            nc.vector.tensor_tensor(out=onehot[:].rearrange("p e t -> p t e"), in0=over_tiles(expert_m8[:]),
                                    in1=over_experts(first[:]), op=ALU.is_equal).then_inc(onehot_ready, 1)
            dve.wait_ge(gate_exp, 1)
            link(nc.vector.tensor_reduce(best[:], work_b[:], AX.X, ALU.add))
            link(nc.vector.reciprocal(first[:], best[:]))
            link(nc.vector.tensor_scalar(gate[:], first[:], tanh_g[:, 1:2], None, ALU.mult))
            dve.wait_ge(ranks_psum, 1)
            link(nc.vector.tensor_tensor_scan(cum[:], ones_wide[:], ps_q[1][:, 0:E * NT], 0.0, ALU.mult, ALU.add))
            nc.vector.memset(starts[:, 0:1], 0.0)
            nc.vector.memset(bounds[:, 0:1], 0.0)
            link(nc.vector.tensor_copy(starts[:, 1:E + 1], cum[:].rearrange("p (e t) -> p e t", t=NT)[:, :, NT - 1]))
            link(nc.vector.scalar_tensor_tensor(out=counts_i[:], in0=starts[:, 1:E + 1], scalar=float(P - 1),
                                                in1=starts[:, 0:E], op0=ALU.add, op1=ALU.subtract))
            link(nc.vector.tensor_scalar(tiles_i[:], counts_i[:], 7, None, ALU.arith_shift_right))
            link(nc.vector.tensor_scalar(tiles_f[:], tiles_i[:], float(MIN_TILES), None, ALU.max))
            link(nc.vector.tensor_tensor_scan(bounds[:, 1:E + 1], ones_wide[:, 0:E], tiles_f[:], 0.0, ALU.mult, ALU.add))
            link(nc.vector.scalar_tensor_tensor(out=shift[:], in0=bounds[:, 0:E], scalar=float(P), in1=starts[:, 0:E],
                                                op0=ALU.mult, op1=ALU.subtract))
            wa = work_a[:].rearrange("p t e -> p (t e)")
            wa_et = wa.rearrange("p (e t) -> p e t", t=NT)
            link(nc.vector.tensor_tensor(out=wa, in0=cum[:], in1=ps_q[1][:, 0:E * NT], op=ALU.subtract))
            link(nc.vector.tensor_tensor(out=cum[:], in0=wa, in1=ps_q[0][:, 0:E * NT], op=ALU.add))
            link(nc.vector.tensor_tensor(out=wa_et, in0=cum[:].rearrange("p (e t) -> p e t", t=NT),
                                         in1=shift[:].unsqueeze(2).to_broadcast([P, E, NT]), op=ALU.add))
            link(nc.vector.tensor_tensor(out=wa_et, in0=wa_et, in1=onehot[:], op=ALU.mult))
            link(nc.vector.tensor_reduce(first[:], wa_et.rearrange("p e t -> p t e"), AX.X, ALU.add))
            link(nc.vector.tensor_copy(pos_i[:, 0], first[:]))
            nc.vector.tensor_scalar(pos_i[:, 1], pos_i[:, 0], 7, None, ALU.arith_shift_right)
            link(nc.vector.tensor_scalar(pos_i[:, 2], pos_i[:, 0], P - 1, None, ALU.bitwise_and))
            nc.vector.tensor_copy(pos_f[:], pos_i[:, 1:3]).then_inc(pos_ready, 1)
            dve.wait_ge(pos_ready, 1)
            link(nc.vector.tensor_scalar(tab_w[:, 0], bounds[:, 0:E], part_iota[:], None, ALU.is_le))
            link(nc.vector.tensor_tensor(out=tab_w[:, 1], in0=tab_w[:, 0], in1=bounds[:, 0:E], op=ALU.mult))
            nc.vector.tensor_reduce(tab_k[:, 0:1], tab_w[:, 0], AX.X, ALU.add)
            link(nc.vector.tensor_reduce(tab[:, 1:2], tab_w[:, 1], AX.X, ALU.max))
            link(nc.vector.tensor_tensor(out=tab_k[:, 1:2], in0=part_iota[:], in1=tab[:, 1:2], op=ALU.subtract))
            link(nc.vector.scalar_tensor_tensor(out=tab_k[:, 2:3], in0=tab_k[:, 0:1], scalar=float(PIECES),
                                                in1=tab_k[:, 1:2], op0=ALU.mult, op1=ALU.add))
            link(nc.vector.scalar_tensor_tensor(out=tab_k[:, 2:3], in0=tab_k[:, 1:2], scalar=float(PIECES),
                                                in1=tab_k[:, 2:3], op0=ALU.is_lt, op1=ALU.mult))
            nc.vector.tensor_scalar(tab[:, 0:1], tab_k[:, 0:1], -1.0, None, ALU.add)
            nc.vector.tensor_scalar(tab[:, 3:4], bounds[:, E:E + 1], -1.0, None, ALU.add)
            nc.vector.scalar_tensor_tensor(out=tab[:, 2:3], in0=tab_k[:, 2:3], scalar=float(E * PIECES),
                                           in1=tab_k[:, 2:3], op0=ALU.is_lt, op1=ALU.mult).then_inc(tab_ready, 1)
            for n in range(NB):
                batch = slice(n * HOT, (n + 1) * HOT)
                if n == 0:
                    nc.vector.tensor_tensor(out=slot_hot[:, batch], in0=slot_iota[:].unsqueeze(1).to_broadcast([P, HOT, P]),
                                            in1=pos_f[:, 1, batch].unsqueeze(2).to_broadcast([P, HOT, P]), op=ALU.is_equal)
                link(nc.vector.tensor_tensor(out=tile_eq[:], in0=col_of_tile[:].unsqueeze(1).to_broadcast([P, HOT, COLS]),
                                             in1=pos_f[:, 0, batch].unsqueeze(2).to_broadcast([P, HOT, COLS]),
                                             op=ALU.is_equal))
                for v, value in enumerate((token_mN, gate)):
                    last = nc.vector.tensor_tensor(out=tile_hot[:, batch, v], in0=tile_eq[:],
                                                   in1=value[:, batch].unsqueeze(2).to_broadcast([P, HOT, COLS]),
                                                   op=ALU.mult)
                last.then_inc(tile_hot_ready, 1)
                dve.wait_ge(tile_hot_ready, n + 1)
            dve.wait_ge(lists_step, 1)
            nc.vector.tensor_scalar(idx_gather[:], ps_s[:, 0:COLS], float(N), float(N - 1), ALU.add, ALU.min).then_inc(lists_ready, 1)
            nc.vector.tensor_scalar(idx_scatter[:], ps_s[:, 0:COLS], float(N), None, ALU.add)
            nc.vector.tensor_copy(gate_sorted[:], ps_s[:, COLS:2 * COLS]).then_inc(lists_ready, 1)

            dve.wait_ge(lists_ready, 2)
            dve.wait_ge(tables_ready, 1)
            last_tile = dve.value_load(last_sorted[:, 0:1], min_val=E * MIN_TILES - 1, max_val=MAXT - 1)
            total = dve.snap(last_tile + 1)

            def norm(t):
                dve.wait_ge(gathered, t * 16 + 16)
                if not (isinstance(t, int) and t == 0):
                    dve.wait_ge(xt_psum, t)
                nc.vector.tensor_scalar(x_norm[:], x_sorted[:, 0:D], x_sorted[:, D + 1:D + 2], x_sorted[:, D:D + 1],
                                        ALU.mult, ALU.subtract).then_inc(xnorm_ready, 1)

            def x_low(t):
                dve.wait_ge(xhi_ready, t + 1)
                nc.vector.tensor_tensor(out=xt_lo[:], in0=px[:, 0:D].rearrange("p (k n) -> p k n", k=DC),
                                        in1=xt_hi[:].bitcast(FP32), op=ALU.subtract).then_inc(xlo_ready, 1)

            def multiply(t, j, start):
                dve.wait_ge(silu_ready[j], t + 1)
                if not start:
                    dve.wait_ge(ht_psum[j], t)
                nc.vector.tensor_tensor(out=hidden[:, j], in0=pg[j][:], in1=silu[:, j], op=ALU.mult
                                        ).then_inc(hidden_ready[j], 1)

            def h_low(t, j):
                dve.wait_ge(hhi_ready[j], t + 1)
                nc.vector.tensor_tensor(out=ht_lo[:, j], in0=ph[j][:], in1=ht_hi[:, j].bitcast(FP32),
                                        op=ALU.subtract).then_inc(hlo_ready[j], 1)

            def finish(t):
                if not (isinstance(t, int) and t == 0):
                    dve.wait_ge(scattered, t * 16)
                dve.wait_ge(down_psum[1], t + 2)
                nc.vector.scalar_tensor_tensor(out=out_tile[:], in0=py[:, 0:D], scalar=gate_sorted[:, bass.ds(t, 1)],
                                               in1=residual[:, bass.ds((t & (RES - 1)) * D, D)], op0=ALU.mult,
                                               op1=ALU.add).then_inc(out_ready, 1)

            def tile(t, start):
                multiply(t, 0, start)
                norm(t + 1)
                x_low(t + 1)
                multiply(t, 1, start)
                h_low(t, 0)
                if not start:
                    finish(t - 1)
                h_low(t, 1)

            dve.sem_inc(out_ready, 1)
            norm(0)
            x_low(0)
            tile(0, True)
            tile(1, False)
            with dve.Fori(2, total) as t:
                tile(t, False)
            finish(last_tile)

        @block.tensor
        def _(pe):
            mm = nc.tensor.matmul
            pe.wait_ge(proj_loaded, 80)
            pe.wait_ge(consts_ready, 1)
            for k in range(DC):
                for oc in range(DC):
                    last = nc.tensor.transpose(ps_q[0][:, k * D + oc * P:k * D + (oc + 1) * P],
                                               w2_in[:, oc, k * P:(k + 1) * P], ident[:])
            last.then_inc(prep_pe, 1)
            for dc in range(DC):
                for b in range(B):
                    last = nc.tensor.transpose(ps_x[dc][:, b * KEYS:(b + 1) * KEYS], ctx_in[:, b, dc * P:(dc + 1) * P],
                                               ident[0:KEYS, 0:KEYS])
            last.then_inc(prep_pe, 1)
            pe.wait_ge(misc_loaded, 80)
            pe.wait_ge(consts_ready, 2)
            for k in range(DC):
                last = mm(ps_o[:, 1, 0:E], mean_of[:], router_in[:, k], start=k == 0, stop=k == DC - 1)
            last.then_inc(prep_pe, 1)
            pe.wait_ge(prep_sb, 3)
            for oc in range(DC):
                for k in range(DC):
                    mm(ps_l[:, oc:oc + 1], w2_t[:, k, oc * P:(oc + 1) * P], b1_in[:, k:k + 1], start=k == 0,
                       stop=k == DC - 1)
            for dc in range(DC):
                for k in range(DC):
                    last = mm(ps_p[:, dc * D:(dc + 1) * D], w1_in[:, k, dc * P:(dc + 1) * P], w2_t[:, k], start=k == 0,
                              stop=k == DC - 1)
            last.then_inc(prep_pe, 1)
            pe.wait_ge(prep_dve, 3)
            for oc in range(DC):
                for k in range(DC):
                    last = mm(ps_s[:, oc * D:(oc + 1) * D], w2_t[:, k, oc * P:(oc + 1) * P], w1_c[:, k], start=k == 0,
                              stop=k == DC - 1)
            last.then_inc(prep_pe, 1)
            pe.wait_ge(mt_ready, 1)
            for oc in range(DC):
                for k in range(DC):
                    last = mm(ps_q[oc][:, 0:KB], m_t[:, k, oc * P:(oc + 1) * P], ctx_t[:, k], start=k == 0, stop=k == DC - 1)
            last.then_inc(prep_pe, 1)
            pe.wait_ge(prep_sb, 6)
            pe.wait_ge(prep_dve, 5)
            for k in range(DC):
                last = mm(ps_o[:].rearrange("p a d -> p (a d)")[:, 0:KB], bq_wide[:, k], kp_t[:, k], start=k == 0,
                          stop=k == DC - 1)
            last.then_inc(prep_pe, 1)
            for dc in range(DC):
                for k in range(DC):
                    last = mm(ps_x[dc][:, 0:KB], m_c[:, k, dc * P:(dc + 1) * P], kp_t[:, k], start=k == 0, stop=k == DC - 1)
            last.then_inc(prep_pe, 1)

            def transpose_tokens(g):
                pe.wait_ge(x_loaded[g % XR], 16 * (g // XR + 1))
                if g:
                    pe.wait_ge(xt1_ready, g)
                for k in range(DC):
                    for b in range(B):
                        last = nc.tensor.transpose(ps_q[k][:, b * P:(b + 1) * P], x_in[:, g % XR, b, k * P:(k + 1) * P],
                                                   ident[:])
                last.then_inc(xt1_psum, 1)

            def transpose_probs(g):
                pe.wait_ge(probs_ready, g + 1)
                if g:
                    pe.wait_ge(pt_ready, g)
                for b in range(B):
                    last = nc.tensor.transpose(ps_p[0:KEYS, b * P:(b + 1) * P], probs[:, g % 2, b], ident[:])
                last.then_inc(pt_psum, 1)

            def transpose_x1(g):
                pe.wait_ge(x1_ready, 2 * (g + 1))
                if g:
                    pe.wait_ge(x1t_ready, g)
                for k in range(DC):
                    for b in range(B):
                        last = nc.tensor.transpose(ps_x[k][:, b * P:(b + 1) * P], x_row[:, g % 2, b, k * P:(k + 1) * P],
                                                   ident[:])
                last.then_inc(x1t_psum, 1)

            def scores(g):
                pe.wait_ge(xt1_ready, g + 1)
                if g:
                    pe.wait_ge(masked_ready, g)
                for b in range(B):
                    for k in range(DC):
                        last = mm(ps_s[:, b * KEYS:(b + 1) * KEYS], x_t[:, k, b * P:(b + 1) * P],
                                  keys_t[:, k, b * KEYS:(b + 1) * KEYS], start=k == 0, stop=k == DC - 1)
                last.then_inc(scores_psum, 1)

            def attend(g, half):
                if half == 0:
                    pe.wait_ge(pt_ready, g + 1)
                if g or half:
                    pe.wait_ge(x1_ready, 2 * g + half)
                for b in range(2 * half, 2 * half + 2):
                    last = mm(ps_o[:, b % 2], probs_t[:, b * P:(b + 1) * P], values[:, b], start=True, stop=True)
                last.then_inc(attn_psum, 1)

            def route_logits(g):
                pe.wait_ge(x1t_ready, g + 1)
                if g:
                    pe.wait_ge(logits_ready, g)
                for b in range(B):
                    for k in range(DC):
                        last = mm(ps_l[:, b * E:(b + 1) * E], x1_t[:, k, b * P:(b + 1) * P], router_c[:, k],
                                  start=k == 0, stop=k == DC - 1)
                last.then_inc(logits_psum, 1)

            pe.wait_ge(prep_sb, 8)
            for i in range(1, NG + 3):
                if i - 1 < NG:
                    transpose_tokens(i - 1)
                if 0 <= i - 2 < NG:
                    transpose_probs(i - 2)
                if 0 <= i - 3 < NG:
                    transpose_x1(i - 3)
                if i - 1 < NG:
                    scores(i - 1)
                if 0 <= i - 2 < NG:
                    attend(i - 2, 0)
                if 0 <= i - 3 < NG:
                    route_logits(i - 3)
                if 0 <= i - 2 < NG:
                    attend(i - 2, 1)

            pe.wait_ge(onehot_ready, 1)
            pe.wait_ge(consts_ready, 3)
            hot = onehot[:].rearrange("p e t -> p (e t)")
            mm(ps_q[0][:, 0:E * NT], before[:], hot, start=True, stop=True)
            mm(ps_q[1][:, 0:E * NT], ones[:], hot, start=True, stop=True).then_inc(ranks_psum, 1)
            pe.wait_ge(tab_ready, 1)
            nc.tensor.transpose(ps_l[0:4, 0:P], tab[:], ident[:]).then_inc(tab_psum, 1)
            for n in range(NB):
                if 0 < n < NB - 1:
                    pe.wait_ge(act_slot_hot, n)
                elif n:
                    pe.wait_ge(pool_slot_hot, 1)
                pe.wait_ge(tile_hot_ready, n + 1)
                for t in range(n * HOT, (n + 1) * HOT):
                    last = mm(ps_s[:, 0:2 * COLS], slot_hot[:, t], tile_hot[:, t].rearrange("p v c -> p (v c)"),
                              start=t == 0, stop=t == NT - 1)
            last.then_inc(lists_step, 1)

            pe.wait_ge(lists_ready, 2)
            pe.wait_ge(tables_ready, 1)
            last_tile = pe.value_load(last_sorted[:, 0:1], min_val=E * MIN_TILES - 1, max_val=MAXT - 1)
            total = pe.snap(last_tile + 1)

            def transpose_x(t):
                pe.wait_ge(xnorm_ready, t + 1)
                for k in range(DC):
                    last = nc.tensor.transpose(px[:, k * P:(k + 1) * P], x_norm[:, k * P:(k + 1) * P], ident[:])
                last.then_inc(xt_psum, 1)

            def up(t, j, slot):
                if j == 0:
                    pe.wait_ge(xlo_ready, t + 1)
                n = 0
                for k in range(DC):
                    for xt, ws in ((xt_hi, (w_hi, w_lo)), (xt_lo, (w_hi,))):
                        for w in ws:
                            for ps, col in ((pa[j], j * HALF), (pg[j], F + j * HALF)):
                                last = mm(ps[:], xt[:, k], w[:, bass.ds(slot + (k * PW + col), HALF)], start=n == 0,
                                          stop=n == 3 * DC - 1)
                            n += 1
                last.then_inc(up_psum[j], 1)

            def transpose_h(t, j, start=False):
                pe.wait_ge(hidden_ready[j], t + 1)
                if j == 0 and not start:
                    pe.wait_ge(hlo_ready[0], t)
                for c in range(HC):
                    last = nc.tensor.transpose(ph[j][:, c * P:(c + 1) * P], hidden[:, j, c * P:(c + 1) * P], ident[:])
                last.then_inc(ht_psum[j], 1)

            def down(t, j, slot):
                n = 0
                for c in range(HC):
                    for ht, ws in ((ht_hi, (w_hi, w_lo)), (ht_lo, (w_hi,))):
                        for w in ws:
                            last = mm(py[:, 0:D], ht[:, j, c * P:(c + 1) * P],
                                      w[:, bass.ds(slot + (DC * PW + (j * HC + c) * D), D)],
                                      start=j == 0 and n == 0, stop=j == 1 and n == 3 * HC - 1)
                            n += 1
                last.then_inc(down_psum[j], 1)

            pe.sem_inc(down_psum[1], 1)
            transpose_x(0)
            pe.wait_ge(w_ready, PIECES)
            up(0, 0, 0)
            up(0, 1, 0)
            transpose_x(1)
            transpose_h(0, 0, start=True)
            expert_now = pe.alloc_register("expert_now")
            expert_old = pe.alloc_register("expert_old")
            pe.reg_mov(expert_now, 0)
            pe.reg_mov(expert_old, 0)
            with pe.Fori(1, total) as t:
                now = pe.snap(expert_now)
                old = pe.snap(expert_old)
                pe.wait_ge(w_ready, now * PIECES + DC)
                up(t, 0, (now & 1) * EW)
                transpose_h(t - 1, 1)
                up(t, 1, (now & 1) * EW)
                following = pe.value_load(tile_expert[:, bass.ds(t + 1, 1)], min_val=0, max_val=E - 1)
                transpose_x(t + 1)
                transpose_h(t, 0)
                pe.wait_ge(out_ready, t)
                pe.wait_ge(w_ready, old * PIECES + PIECES)
                down(t - 1, 0, (old & 1) * EW)
                pe.wait_ge(hlo_ready[1], t)
                down(t - 1, 1, (old & 1) * EW)
                pe.reg_mov(expert_old, now)
                pe.reg_mov(expert_now, following)
            old = pe.snap(expert_old)
            transpose_h(last_tile, 1)
            pe.wait_ge(hlo_ready[0], last_tile + 1)
            pe.wait_ge(out_ready, last_tile + 1)
            pe.wait_ge(w_ready, old * PIECES + PIECES)
            down(last_tile, 0, (old & 1) * EW)
            pe.wait_ge(hlo_ready[1], last_tile + 1)
            down(last_tile, 1, (old & 1) * EW)


_INS = ['x', 'ctx_1024', 'fside_1xSxS2_0', 'g_xattn', 'g_ffn', 'L0_xattn_W1', 'L0_xattn_b1', 'L0_xattn_W2',
        'L0_xattn_b2', 'L0_ffn_router_w', 'L0_ffn_router_b', 'L0_ffn_w1', 'L0_ffn_w2']


def kernel(**inputs):
    import numpy as np
    import concourse.bacc as bacc
    from concourse.bass_utils import run_bass_kernel_spmd

    nc = bacc.Bacc("TRN2", target_bir_lowering=False, num_devices=1)
    arrays, args = {}, []
    for name in _INS:
        a = np.ascontiguousarray(inputs[name])
        arrays[f"in_{name}"] = a
        args.append(nc.dram_tensor(f"in_{name}", a.shape, mybir.dt.from_np(a.dtype), kind="ExternalInput").ap())
    x = inputs["x"]
    args.append(nc.dram_tensor("out_0", x.shape, mybir.dt.from_np(np.dtype("float32")), kind="ExternalOutput").ap())
    flamingo_block(nc, *args)
    r = run_bass_kernel_spmd(nc, [arrays], core_ids=[0])
    return r.results[0]["out_0"]
```
